# Optimizing a Trainium2 kernel written in Bass

```python
import numpy as np
import jax
import jax.numpy as jnp

def _softmax(x, axis=-1):
    return jax.nn.softmax(x, axis=axis)

def _gelu(x):
    return jax.nn.gelu(x, approximate=True)

def _silu(x):
    return jax.nn.silu(x)

def _sigmoid(x):
    return jax.nn.sigmoid(x)

def _layernorm(x, axis=-1, eps=1e-05):
    m = jnp.mean(x, axis=axis, keepdims=True)
    v = jnp.var(x, axis=axis, keepdims=True)
    return (x - m) / jnp.sqrt(v + eps)

def _scatter_add(tgt, idx, src, axis=0):
    return tgt.at[idx].add(src)

def _segment_sum(src, seg, n):
    return jax.ops.segment_sum(src, seg, n)
kernel_name = 'mk_decoder_preln_d2_seqx_r8_05be36'

def setup_inputs(seed: int=0):
    np.random.seed(seed)
    _w = jnp.asarray

    def _rec_inputs():
        import jax
        import jax.numpy as jnp
        _rk = jax.random.key(seed)
        x = -0.0003929 + 0.9999 * jax.random.normal(jax.random.fold_in(_rk, 1), (16, 64, 256), jnp.float32)
        _lenS = 64 - jax.random.randint(jax.random.fold_in(_rk, 7), (16,), 0, max(1, 64 // 4) + 1, jnp.int32)
        _lenS2 = 64 - jax.random.randint(jax.random.fold_in(_rk, 8), (16,), 0, max(1, 64 // 4) + 1, jnp.int32)
        _ctx_1024P = jax.random.normal(jax.random.fold_in(_rk, 11), (16, 16, 128), jnp.float32)
        _ctx_1024c = jax.random.dirichlet(jax.random.fold_in(_rk, 511), 0.3 * jnp.ones((16,), jnp.float32), (16, 64))
        _ctx_1024t = jnp.einsum('bsk,bkd->bsd', _ctx_1024c, _ctx_1024P)
        _ctx_1024t = _ctx_1024t * jax.lax.rsqrt(jnp.mean(jnp.square(_ctx_1024t)) + 1e-12) * 0.953939
        ctx_1024 = 0.000227908 + 0.99994 * (_ctx_1024t + 0.3 * jax.random.normal(jax.random.fold_in(_rk, 611), (16, 64, 128), jnp.float32))
        _validS = jnp.arange(64)[None, :] < _lenS[:, None]
        _validS2 = jnp.arange(64)[None, :] < _lenS2[:, None]
        _causal = jnp.tril(jnp.ones((64, 64), dtype=bool))
        mask_BxS2_bf1 = jnp.ones((16, 64), dtype=bool)
        return (x, ctx_1024, mask_BxS2_bf1)
    x, ctx_1024, mask_BxS2_bf1 = _rec_inputs()

    def _L0_attn_setup():
        import jax, jax.numpy as jnp
        import numpy as np
        D_MODEL = 256
        D_INNER = 512
        D_XB = 64
        D_STATE = 16
        D_CONV = 4
        DT_RANK = 128
        BATCH = 2
        SEQLEN = 128
        NXB = D_XB // D_STATE
        NC = D_INNER // D_STATE
        REP = NC // NXB
        DPG = D_INNER // NC

        def _mamba_fwd(hidden_states, W_in, W_dt, b_dt, conv_w, conv_b, A_log, D_param, W_out):
            b, l, _ = hidden_states.shape
            A = -jnp.exp(A_log)
            zxbcdt = hidden_states @ W_in.T
            splits = np.cumsum([D_INNER, D_XB, D_XB, D_INNER])
            z, x, Bm, Cm, dtl = jnp.split(zxbcdt, splits, axis=-1)
            dt_full = dtl @ W_dt.T + b_dt
            delta = jax.nn.softplus(dt_full + b_dt)
            x = x.transpose(0, 2, 1).reshape(b, NXB, D_STATE, l)
            x = jnp.repeat(x, REP, axis=1).reshape(b, D_INNER, l)
            x = jax.lax.conv_general_dilated(x, conv_w, (1,), [(D_CONV - 1, 0)], dimension_numbers=('NCH', 'OIH', 'NCH'), feature_group_count=D_INNER)
            x = jax.nn.silu(x + conv_b[None, :, None])
            Bg = jnp.repeat(Bm.reshape(b, l, NXB, D_STATE), REP, axis=2)
            Cg = Cm.reshape(b, l, NC, D_STATE)
            u_t = x.transpose(2, 0, 1)
            d_t = delta.transpose(1, 0, 2)
            B_t = Bg.transpose(1, 0, 2, 3)
            C_t = Cg.transpose(1, 0, 2, 3)
            A_g = A.reshape(NC, DPG, D_STATE)

            def step(state, inp):
                u, dlt, Bs, Cs = inp
                dA = jnp.exp(dlt.reshape(b, NC, DPG)[..., None] * A_g)
                du = (dlt * u).reshape(b, NC, DPG)
                state = dA * state + du[..., None] * Bs[:, :, None, :]
                y = jnp.einsum('bgdn,bgn->bgd', state, Cs).reshape(b, D_INNER)
                return (state, y)
            init = jnp.zeros((b, NC, DPG, D_STATE), jnp.float32)
            _, ys = jax.lax.scan(step, init, (u_t, d_t, B_t, C_t))
            y = ys.transpose(1, 0, 2)
            y = y + x.transpose(0, 2, 1) * D_param
            y = y * jax.nn.silu(z)
            return y @ W_out.T
        key = jax.random.key(seed)
        ks = jax.random.split(key, 8)
        s = 0.02
        hidden_states = jax.random.normal(ks[0], (BATCH, SEQLEN, D_MODEL), jnp.float32)
        W_in = jax.random.normal(ks[1], (2 * D_XB + 2 * D_INNER + DT_RANK, D_MODEL), jnp.float32) * s
        dt_std = DT_RANK ** (-0.5)
        W_dt = jax.random.uniform(ks[2], (D_INNER, DT_RANK), jnp.float32, -dt_std, dt_std)
        dt = jnp.exp(jax.random.uniform(ks[3], (D_INNER,), jnp.float32) * (np.log(0.1) - np.log(0.001)) + np.log(0.001))
        dt = jnp.clip(dt, 0.0001)
        b_dt = dt + jnp.log(-jnp.expm1(-dt))
        conv_w = jax.random.normal(ks[4], (D_INNER, 1, D_CONV), jnp.float32) * D_CONV ** (-0.5)
        conv_b = jnp.zeros((D_INNER,), jnp.float32)
        A_log = jnp.log(jnp.tile(jnp.arange(1, D_STATE + 1, dtype=jnp.float32), (D_INNER, 1)))
        D_param = jnp.ones((D_INNER,), jnp.float32)
        W_out = jax.random.normal(ks[5], (D_MODEL, D_INNER), jnp.float32) * s
        return dict(hidden_states=hidden_states, W_in=W_in, W_dt=W_dt, b_dt=b_dt, conv_w=conv_w, conv_b=conv_b, A_log=A_log, D_param=D_param, W_out=W_out)
    _L0_attn_all = _L0_attn_setup()
    _L0_attn_in = {k: v for k, v in _L0_attn_all.items() if k in ('W_in', 'W_dt', 'b_dt', 'conv_w', 'conv_b', 'A_log', 'D_param', 'W_out')}
    del _L0_attn_all

    def _L0_xattn_setup():
        import jax, jax.numpy as jnp
        import numpy as np
        EPS = 1e-05

        def rmsnorm(x, g, eps=EPS):
            var = jnp.mean(jnp.square(x), axis=-1, keepdims=True)
            return x * jax.lax.rsqrt(var + eps) * g
        key = jax.random.key(seed)
        ks = jax.random.split(key, 8)
        B, Sq, Skv = (2, 512, 64)
        dim, cdim, H, D = (256, 128, 16, 128)
        inner = H * D
        s = lambda f: 1.0 / np.sqrt(f)
        return {'hidden_states': jax.random.normal(ks[0], (B, Sq, dim), jnp.float32), 'encoder_hidden_states': jax.random.normal(ks[1], (B, Skv, cdim), jnp.float32), 'Wq': jax.random.normal(ks[2], (dim, inner), jnp.float32) * s(dim), 'Wk': jax.random.normal(ks[3], (cdim, inner), jnp.float32) * s(cdim), 'Wv': jax.random.normal(ks[4], (cdim, inner), jnp.float32) * s(cdim), 'Wo': jax.random.normal(ks[5], (inner, dim), jnp.float32) * s(inner), 'gq': jnp.ones((D,), jnp.float32), 'gk': jnp.ones((D,), jnp.float32)}
    _L0_xattn_all = _L0_xattn_setup()
    _L0_xattn_in = {k: v for k, v in _L0_xattn_all.items() if k in ('Wq', 'Wk', 'Wv', 'Wo', 'gq', 'gk')}
    del _L0_xattn_all

    def _L0_ffn_setup():
        import jax, jax.numpy as jnp
        import numpy as np
        DIM = 256
        HIDDEN = 1024
        NUM_EXPERTS = 2
        BATCH, SEQ = (4, 128)
        key = jax.random.key(seed)
        k1, k2, k3, k4 = jax.random.split(key, 4)
        x = jax.random.normal(k1, (BATCH, SEQ, DIM), dtype=jnp.float32)
        w_router = jax.random.normal(k2, (NUM_EXPERTS, DIM), dtype=jnp.float32) * (1.0 / np.sqrt(DIM))
        w_fc = jax.random.normal(k3, (NUM_EXPERTS, HIDDEN, DIM), dtype=jnp.float32) * (1.0 / np.sqrt(DIM))
        w_proj = jax.random.normal(k4, (NUM_EXPERTS, DIM, HIDDEN), dtype=jnp.float32) * (1.0 / np.sqrt(HIDDEN))
        return {'x': x, 'w_router': w_router, 'w_fc': w_fc, 'w_proj': w_proj}
    _L0_ffn_all = _L0_ffn_setup()
    _L0_ffn_in = {k: v for k, v in _L0_ffn_all.items() if k in ('w_router', 'w_fc', 'w_proj')}
    del _L0_ffn_all

    def _L1_attn_setup():
        import jax, jax.numpy as jnp
        import numpy as np
        D_MODEL = 256
        N_HEADS = 16
        SEQ_LEN = 256
        BATCH = 2
        BIAS_MAX = 8.0

        def alibi_bias(n_heads, seq_len, dtype):
            pos = jnp.arange(1 - seq_len, 1, dtype=dtype)
            m = jnp.arange(1, n_heads + 1, dtype=dtype) * (BIAS_MAX / n_heads)
            slopes = 1.0 / 2.0 ** m
            return pos[None, :] * slopes[:, None]
        key = jax.random.key(seed)
        k1, k2, k3 = jax.random.split(key, 3)
        s = 1.0 / np.sqrt(D_MODEL)
        x = jax.random.normal(k1, (BATCH, SEQ_LEN, D_MODEL), dtype=jnp.float32)
        Wqkv = jax.random.normal(k2, (3 * D_MODEL, D_MODEL), dtype=jnp.float32) * s
        b_qkv = jnp.zeros((3 * D_MODEL,), dtype=jnp.float32)
        Wout = jax.random.normal(k3, (D_MODEL, D_MODEL), dtype=jnp.float32) * s
        b_out = jnp.zeros((D_MODEL,), dtype=jnp.float32)
        return {'x': x, 'Wqkv': Wqkv, 'b_qkv': b_qkv, 'Wout': Wout, 'b_out': b_out}
    _L1_attn_all = _L1_attn_setup()
    _L1_attn_in = {k: v for k, v in _L1_attn_all.items() if k in ('Wqkv', 'b_qkv', 'Wout', 'b_out')}
    del _L1_attn_all

    def _L1_xattn_setup():
        import jax, jax.numpy as jnp
        import numpy as np
        N_HEADS = 16
        N_KV_HEADS = 8
        HEAD_DIM = 128
        D_TEXT = 256
        D_VISION = 128
        GROUPS = N_HEADS // N_KV_HEADS
        key = jax.random.key(seed)
        ks = jax.random.split(key, 6)
        B, T_text, T_vis = (4, 256, 72)
        text_hidden = jax.random.normal(ks[0], (B, T_text, D_TEXT), dtype=jnp.float32)
        vision_tokens = jax.random.normal(ks[1], (B, T_vis, D_VISION), dtype=jnp.float32)
        vision_mask = jnp.ones((B, T_vis), dtype=bool)
        s = 0.02
        Wq = jax.random.normal(ks[2], (D_TEXT, N_HEADS * HEAD_DIM), dtype=jnp.float32) * s
        Wk = jax.random.normal(ks[3], (D_VISION, N_KV_HEADS * HEAD_DIM), dtype=jnp.float32) * s
        Wv = jax.random.normal(ks[4], (D_VISION, N_KV_HEADS * HEAD_DIM), dtype=jnp.float32) * s
        Wo = jax.random.normal(ks[5], (N_HEADS * HEAD_DIM, D_TEXT), dtype=jnp.float32) * s
        return {'text_hidden': text_hidden, 'vision_tokens': vision_tokens, 'vision_mask': vision_mask, 'Wq': Wq, 'Wk': Wk, 'Wv': Wv, 'Wo': Wo}
    _L1_xattn_all = _L1_xattn_setup()
    _L1_xattn_in = {k: v for k, v in _L1_xattn_all.items() if k in ('Wq', 'Wk', 'Wv', 'Wo')}
    del _L1_xattn_all

    def _L1_ffn_setup():
        import jax, jax.numpy as jnp
        import numpy as np
        EPS = 1e-05

        def _quant_weight(w):
            scale = jnp.mean(jnp.abs(w)) + EPS
            wq = jnp.clip(jnp.round(w / scale), -1.0, 1.0)
            return (wq, scale)

        def _quant_act(x):
            s = jnp.max(jnp.abs(x), axis=-1, keepdims=True) / 127.0 + EPS
            xq = jnp.clip(jnp.round(x / s), -128.0, 127.0)
            return (xq, s)

        def _qlinear(x, w):
            wq, ws = _quant_weight(w)
            xq, xs = _quant_act(x)
            y = jnp.einsum('bsi,oi->bso', xq, wq)
            return y * xs * ws
        key = jax.random.key(seed)
        k1, k2, k3, k4 = jax.random.split(key, 4)
        H, I = (256, 1024)
        x = jax.random.normal(k1, (4, 512, H), dtype=jnp.float32)
        w_gate = jax.random.normal(k2, (I, H), dtype=jnp.float32) * (1.0 / np.sqrt(H))
        w_up = jax.random.normal(k3, (I, H), dtype=jnp.float32) * (1.0 / np.sqrt(H))
        w_down = jax.random.normal(k4, (H, I), dtype=jnp.float32) * (1.0 / np.sqrt(I))
        return {'x': x, 'w_gate': w_gate, 'w_up': w_up, 'w_down': w_down}
    _L1_ffn_all = _L1_ffn_setup()
    _L1_ffn_in = {k: v for k, v in _L1_ffn_all.items() if k in ('w_gate', 'w_up', 'w_down')}
    del _L1_ffn_all
    return {'x': x, 'ctx_1024': ctx_1024, 'mask_BxS2_bf1': mask_BxS2_bf1, 'L0_attn_W_in': _L0_attn_in['W_in'], 'L0_attn_W_dt': _L0_attn_in['W_dt'], 'L0_attn_b_dt': _L0_attn_in['b_dt'], 'L0_attn_conv_w': _L0_attn_in['conv_w'], 'L0_attn_conv_b': _L0_attn_in['conv_b'], 'L0_attn_A_log': _L0_attn_in['A_log'], 'L0_attn_D_param': _L0_attn_in['D_param'], 'L0_attn_W_out': _L0_attn_in['W_out'], 'L0_xattn_Wq': _L0_xattn_in['Wq'], 'L0_xattn_Wk': _L0_xattn_in['Wk'], 'L0_xattn_Wv': _L0_xattn_in['Wv'], 'L0_xattn_Wo': _L0_xattn_in['Wo'], 'L0_xattn_gq': _L0_xattn_in['gq'], 'L0_xattn_gk': _L0_xattn_in['gk'], 'L0_ffn_w_router': _L0_ffn_in['w_router'], 'L0_ffn_w_fc': _L0_ffn_in['w_fc'], 'L0_ffn_w_proj': _L0_ffn_in['w_proj'], 'L1_attn_Wqkv': _L1_attn_in['Wqkv'], 'L1_attn_b_qkv': _L1_attn_in['b_qkv'], 'L1_attn_Wout': _L1_attn_in['Wout'], 'L1_attn_b_out': _L1_attn_in['b_out'], 'L1_xattn_Wq': _L1_xattn_in['Wq'], 'L1_xattn_Wk': _L1_xattn_in['Wk'], 'L1_xattn_Wv': _L1_xattn_in['Wv'], 'L1_xattn_Wo': _L1_xattn_in['Wo'], 'L1_ffn_w_gate': _L1_ffn_in['w_gate'], 'L1_ffn_w_up': _L1_ffn_in['w_up'], 'L1_ffn_w_down': _L1_ffn_in['w_down']}

def reference(x, ctx_1024, mask_BxS2_bf1, L0_attn_W_in, L0_attn_W_dt, L0_attn_b_dt, L0_attn_conv_w, L0_attn_conv_b, L0_attn_A_log, L0_attn_D_param, L0_attn_W_out, L0_xattn_Wq, L0_xattn_Wk, L0_xattn_Wv, L0_xattn_Wo, L0_xattn_gq, L0_xattn_gk, L0_ffn_w_router, L0_ffn_w_fc, L0_ffn_w_proj, L1_attn_Wqkv, L1_attn_b_qkv, L1_attn_Wout, L1_attn_b_out, L1_xattn_Wq, L1_xattn_Wk, L1_xattn_Wv, L1_xattn_Wo, L1_ffn_w_gate, L1_ffn_w_up, L1_ffn_w_down):
    import jax
    import jax.numpy as jnp

    def _L0_attn_ref(hidden_states, W_in, W_dt, b_dt, conv_w, conv_b, A_log, D_param, W_out):
        import jax, jax.numpy as jnp
        import numpy as np
        D_MODEL = 256
        D_INNER = 512
        D_XB = 64
        D_STATE = 16
        D_CONV = 4
        DT_RANK = 128
        BATCH = 2
        SEQLEN = 128
        NXB = D_XB // D_STATE
        NC = D_INNER // D_STATE
        REP = NC // NXB
        DPG = D_INNER // NC

        def _mamba_fwd(hidden_states, W_in, W_dt, b_dt, conv_w, conv_b, A_log, D_param, W_out):
            b, l, _ = hidden_states.shape
            A = -jnp.exp(A_log)
            zxbcdt = hidden_states @ W_in.T
            splits = np.cumsum([D_INNER, D_XB, D_XB, D_INNER])
            z, x, Bm, Cm, dtl = jnp.split(zxbcdt, splits, axis=-1)
            dt_full = dtl @ W_dt.T + b_dt
            delta = jax.nn.softplus(dt_full + b_dt)
            x = x.transpose(0, 2, 1).reshape(b, NXB, D_STATE, l)
            x = jnp.repeat(x, REP, axis=1).reshape(b, D_INNER, l)
            x = jax.lax.conv_general_dilated(x, conv_w, (1,), [(D_CONV - 1, 0)], dimension_numbers=('NCH', 'OIH', 'NCH'), feature_group_count=D_INNER)
            x = jax.nn.silu(x + conv_b[None, :, None])
            Bg = jnp.repeat(Bm.reshape(b, l, NXB, D_STATE), REP, axis=2)
            Cg = Cm.reshape(b, l, NC, D_STATE)
            u_t = x.transpose(2, 0, 1)
            d_t = delta.transpose(1, 0, 2)
            B_t = Bg.transpose(1, 0, 2, 3)
            C_t = Cg.transpose(1, 0, 2, 3)
            A_g = A.reshape(NC, DPG, D_STATE)

            def step(state, inp):
                u, dlt, Bs, Cs = inp
                dA = jnp.exp(dlt.reshape(b, NC, DPG)[..., None] * A_g)
                du = (dlt * u).reshape(b, NC, DPG)
                state = dA * state + du[..., None] * Bs[:, :, None, :]
                y = jnp.einsum('bgdn,bgn->bgd', state, Cs).reshape(b, D_INNER)
                return (state, y)
            init = jnp.zeros((b, NC, DPG, D_STATE), jnp.float32)
            _, ys = jax.lax.scan(step, init, (u_t, d_t, B_t, C_t))
            y = ys.transpose(1, 0, 2)
            y = y + x.transpose(0, 2, 1) * D_param
            y = y * jax.nn.silu(z)
            return y @ W_out.T
        return _mamba_fwd(hidden_states, W_in, W_dt, b_dt, conv_w, conv_b, A_log, D_param, W_out)

    def _L0_xattn_ref(hidden_states, encoder_hidden_states, Wq, Wk, Wv, Wo, gq, gk):
        import jax, jax.numpy as jnp
        import numpy as np
        EPS = 1e-05

        def rmsnorm(x, g, eps=EPS):
            var = jnp.mean(jnp.square(x), axis=-1, keepdims=True)
            return x * jax.lax.rsqrt(var + eps) * g
        B, Sq, _ = hidden_states.shape
        Skv = encoder_hidden_states.shape[1]
        D = gq.shape[0]
        H = Wq.shape[1] // D
        scale = 1.0 / np.sqrt(D)
        q = (hidden_states @ Wq).reshape(B, Sq, H, D)
        k = (encoder_hidden_states @ Wk).reshape(B, Skv, H, D)
        v = (encoder_hidden_states @ Wv).reshape(B, Skv, H, D)
        q = rmsnorm(q, gq)
        k = rmsnorm(k, gk)
        scores = jnp.einsum('bqhd,bkhd->bhqk', q, k) * scale
        attn = jax.nn.softmax(scores, axis=-1)
        out = jnp.einsum('bhqk,bkhd->bqhd', attn, v)
        out = out.reshape(B, Sq, H * D)
        return out @ Wo

    def _L0_ffn_ref(x, w_router, w_fc, w_proj):
        import jax, jax.numpy as jnp
        import numpy as np
        DIM = 256
        HIDDEN = 1024
        NUM_EXPERTS = 2
        BATCH, SEQ = (4, 128)
        bsz, seq, dim = x.shape
        num_experts = w_router.shape[0]
        x_flat = x.reshape(-1, dim)
        logits = x_flat @ w_router.T
        probs = jax.nn.softmax(logits, axis=-1)
        top_idx = jnp.argmax(probs, axis=-1)
        top_weight = jnp.take_along_axis(probs, top_idx[:, None], axis=1)[:, 0]
        h = jnp.einsum('nd,ehd->enh', x_flat, w_fc)
        a = jnp.square(jnp.where(h >= 0, h, 0.5 * h))
        expert_out = jnp.einsum('enh,edh->end', a, w_proj)
        mask = (top_idx[None, :] == jnp.arange(num_experts)[:, None]).astype(x.dtype)
        out = jnp.einsum('end,en->nd', expert_out, mask * top_weight[None, :])
        return out.reshape(bsz, seq, dim)

    def _L1_attn_ref(x, Wqkv, b_qkv, Wout, b_out):
        import jax, jax.numpy as jnp
        import numpy as np
        D_MODEL = 256
        N_HEADS = 16
        SEQ_LEN = 256
        BATCH = 2
        BIAS_MAX = 8.0

        def alibi_bias(n_heads, seq_len, dtype):
            pos = jnp.arange(1 - seq_len, 1, dtype=dtype)
            m = jnp.arange(1, n_heads + 1, dtype=dtype) * (BIAS_MAX / n_heads)
            slopes = 1.0 / 2.0 ** m
            return pos[None, :] * slopes[:, None]
        B, S, D = x.shape
        H = N_HEADS
        hd = D // H
        scale = 1.0 / jnp.sqrt(jnp.asarray(hd, dtype=x.dtype))
        qkv = x @ Wqkv.T + b_qkv
        q, k, v = jnp.split(qkv, 3, axis=-1)
        q = q.reshape(B, S, H, hd)
        k = k.reshape(B, S, H, hd)
        v = v.reshape(B, S, H, hd)
        scores = jnp.einsum('bqhd,bkhd->bhqk', q, k) * scale
        bias = alibi_bias(H, S, x.dtype)
        scores = scores + bias[None, :, None, :]
        causal = jnp.tril(jnp.ones((S, S), dtype=bool))
        scores = jnp.where(causal[None, None, :, :], scores, jnp.asarray(-1000000000.0, dtype=x.dtype))
        p = jax.nn.softmax(scores, axis=-1)
        ctx = jnp.einsum('bhqk,bkhd->bqhd', p, v).reshape(B, S, D)
        return ctx @ Wout.T + b_out

    def _L1_xattn_ref(text_hidden, vision_tokens, vision_mask, Wq, Wk, Wv, Wo):
        import jax, jax.numpy as jnp
        import numpy as np
        N_HEADS = 16
        N_KV_HEADS = 8
        HEAD_DIM = 128
        D_TEXT = 256
        D_VISION = 128
        GROUPS = N_HEADS // N_KV_HEADS
        B, T_text, _ = text_hidden.shape
        T_vis = vision_tokens.shape[1]
        scale = jnp.float32(np.sqrt(HEAD_DIM))
        q = (text_hidden @ Wq).reshape(B, T_text, N_HEADS, HEAD_DIM).transpose(0, 2, 1, 3)
        k = (vision_tokens @ Wk).reshape(B, T_vis, N_KV_HEADS, HEAD_DIM).transpose(0, 2, 1, 3)
        v = (vision_tokens @ Wv).reshape(B, T_vis, N_KV_HEADS, HEAD_DIM).transpose(0, 2, 1, 3)
        k = jnp.repeat(k, GROUPS, axis=1)
        v = jnp.repeat(v, GROUPS, axis=1)
        scores = jnp.einsum('bhtd,bhsd->bhts', q, k) / scale
        mask = vision_mask[:, None, None, :]
        scores = jnp.where(mask, scores, -jnp.inf)
        attn = jax.nn.softmax(scores, axis=-1)
        attn = jnp.nan_to_num(attn, nan=0.0)
        out = jnp.einsum('bhts,bhsd->bhtd', attn, v)
        out = out.transpose(0, 2, 1, 3).reshape(B, T_text, N_HEADS * HEAD_DIM)
        return out @ Wo

    def _L1_ffn_ref(x, w_gate, w_up, w_down):
        import jax, jax.numpy as jnp
        import numpy as np
        EPS = 1e-05

        def _quant_weight(w):
            scale = jnp.mean(jnp.abs(w)) + EPS
            wq = jnp.clip(jnp.round(w / scale), -1.0, 1.0)
            return (wq, scale)

        def _quant_act(x):
            s = jnp.max(jnp.abs(x), axis=-1, keepdims=True) / 127.0 + EPS
            xq = jnp.clip(jnp.round(x / s), -128.0, 127.0)
            return (xq, s)

        def _qlinear(x, w):
            wq, ws = _quant_weight(w)
            xq, xs = _quant_act(x)
            y = jnp.einsum('bsi,oi->bso', xq, wq)
            return y * xs * ws
        gate = jax.nn.silu(_qlinear(x, w_gate))
        up = _qlinear(x, w_up)
        return _qlinear(gate * up, w_down)
    x = x + _L0_attn_ref(_layernorm(x, axis=-1), L0_attn_W_in, L0_attn_W_dt, L0_attn_b_dt, L0_attn_conv_w, L0_attn_conv_b, L0_attn_A_log, L0_attn_D_param, L0_attn_W_out)
    x = x + _L0_xattn_ref(_layernorm(x, axis=-1), ctx_1024, L0_xattn_Wq, L0_xattn_Wk, L0_xattn_Wv, L0_xattn_Wo, L0_xattn_gq, L0_xattn_gk)
    x = x + _L0_ffn_ref(_layernorm(x, axis=-1), L0_ffn_w_router, L0_ffn_w_fc, L0_ffn_w_proj)
    x = x + _L1_attn_ref(_layernorm(x, axis=-1), L1_attn_Wqkv, L1_attn_b_qkv, L1_attn_Wout, L1_attn_b_out)
    x = x + _L1_xattn_ref(_layernorm(x, axis=-1), ctx_1024, mask_BxS2_bf1, L1_xattn_Wq, L1_xattn_Wk, L1_xattn_Wv, L1_xattn_Wo)
    x = x + _L1_ffn_ref(_layernorm(x, axis=-1), L1_ffn_w_gate, L1_ffn_w_up, L1_ffn_w_down)
    return x

_drawn_inputs = setup_inputs


def setup_inputs(seed=0):
    import zlib

    import numpy as np

    out = dict(_drawn_inputs(seed))
    spreads = {'L0_attn_conv_b': (0.0, 0.359),
     'L0_attn_D_param': (1.0, 0.6),
     'L0_xattn_gq': (1.0, 0.2),
     'L0_xattn_gk': (1.0, 0.2),
     'L1_attn_b_qkv': (0.0, 0.1),
     'L1_attn_b_out': (0.0, 0.1)}
    factors = {'L0_attn_W_dt': 8.0,
     'L0_attn_b_dt': 8.0,
     'L0_attn_A_log': 8.0,
     'L1_xattn_Wq': 8.0,
     'L1_xattn_Wk': 8.0}
    for name, (base, spread) in spreads.items():
        noise = np.random.default_rng([zlib.crc32(name.encode()), seed]).standard_normal(out[name].shape)
        drawn = base * np.exp(spread * noise) if base else spread * noise
        out[name] = jnp.asarray(drawn.astype(out[name].dtype))
    for name, factor in factors.items():
        out[name] = (out[name] * factor).astype(out[name].dtype)
    return out
```

```python
from contextlib import ExitStack

import concourse.bass as bass
from concourse import mybir

F32 = mybir.dt.float32
BF16 = mybir.dt.bfloat16
U8 = mybir.dt.uint8
ALU = mybir.AluOpType
ACT = mybir.ActivationFunctionType
AX = mybir.AxisListType

B, S, D = 16, 64, 256
TOK = B * S
NT = TOK // 128
KH = D // 128
HALF = TOK // 2
EPS = 1e-5
DI, DXB, DST, DCONV, DTR = 512, 64, 16, 4, 128
NK = DI // 128
CD, HD, NH = 128, 128, 16
NKV = 8
HID = 1024
HB = HID // 128
HDS = D // NH
M_X, M_B, M_C, M_DT = DI, 2 * DI, 2 * DI + DXB, 3 * DI + DXB
M_COLS = M_DT + DTR
MAGIC = 1.5 * 2.0 ** 23
NEG = -1e30
QSCALE = float(HD) ** -0.5
LOG1P_SPLIT = 2.0 ** -8


class Counted:

    def __init__(self, sem):
        self.sem, self.n = sem, 0

    def on(self, ins):
        ins.then_inc(self.sem, 1)
        self.n += 1
        return ins


def work_turns(order):
    seen, turns = {"act": 0, "dve": 0}, {}
    for w, (job, by) in enumerate(order):
        seen[by] += 1
        turns[job] = (w, by, seen[by])
    return turns


def program(nc, io, out):
    ctx = ExitStack()
    with ctx:
        def sb(name, shape, dt=F32):
            return ctx.enter_context(nc.sbuf_tensor(name, shape, dt))

        sems = {}

        def sem(name):
            if name not in sems:
                sems[name] = ctx.enter_context(nc.semaphore(name))
            return sems[name]

        ident = sb("ident", [128, 128])
        identb = sb("identb", [128, 128], BF16)
        ones = sb("ones", [128, 128])
        sel_b = sb("sel_b", [96, 32, 128], BF16)
        sel_c = sb("sel_c", [96, 4, 128], BF16)
        x = sb("x", [128, NT, D])
        xn = sb("xn", [128, NT, D])
        xnT = sb("xnT", [128, KH, TOK])
        ctxT = sb("ctxT", [128, TOK])
        ctxn = sb("ctxn", [128, NT, CD])
        stats = sb("stats", [128, NT, 6])
        mv = sb("mv", [128, NT, 2])
        rstd = sb("rstd", [128, NT])
        small = sb("small", [128, 96])
        head_mask = sb("head_mask", [128, 8])
        a_log = sb("a_log", [128, NK, DST])
        mpar = sb("mpar", [128, NK, 8])
        qkb = sb("qkb", [128, 4])
        ps = ctx.enter_context(nc.psum_tensor("ps", [128, 8, 512], F32))
        region = {"A": sb("region_a", [128, 48 * 256]), "B": sb("region_b", [128, 48 * 256]),
                  "C": sb("region_c", [128, 64 * 256])}

        def view(name, kb, shape, dt=F32, rows=128):
            size = 4 if dt == F32 else 2 if dt == BF16 else 1
            n = 1
            for d in shape:
                n *= d
            a = int(kb * 256)
            words = n * size // 4
            v = region[name][0:rows, a:a + words]
            if dt != F32:
                v = v.bitcast(dt)
            if len(shape) == 2:
                v = v.rearrange("p (a b) -> p a b", b=shape[1])
            if len(shape) == 3:
                v = v.rearrange("p (a b c) -> p a b c", b=shape[1], c=shape[2])
            return v

        eps_col = small[:, 0:1]
        one_col = small[:, 1:2]
        zero_col = small[:, 2:3]
        gq_col, gk_col, g_col = small[:, 3:4], small[:, 4:5], small[:, 5:6]

        m_win = view("B", 0, [KH, M_COLS])
        m_wdt = view("B", 14, [DI])
        m_wout = view("B", 16, [NK, D])
        m_sb = view("B", 20, [2, TOK], BF16, 96)
        m_sc = view("B", 24, [4, TOK], BF16, 96)
        m_part = [view("B", 32 + 2 * i, [TOK], BF16) for i in range(3)]
        m_rest = view("B", 38, [TOK])
        m_dtl = view("B", 42, [TOK])
        m_da = [view("C", 4 * i, [B, S]) for i in range(2)]
        m_dbu = [view("C", 8 + 4 * i, [TOK]) for i in range(2)]
        m_h = [view("C", 16 + 4 * i, [TOK]) for i in range(2)]
        m_hc = [view("C", 24 + 4 * i, [TOK]) for i in range(2)]
        m_u = view("C", 32, [TOK])
        m_delta = view("C", 36, [B, S])
        m_du = view("C", 40, [TOK])
        m_zs = view("C", 44, [TOK])
        m_yg = view("C", 48, [NK, TOK])
        wq = view("A", 0, [KH, NH * HD])
        wk = view("A", 16, [NH * HD])
        wvT = view("A", 24, [NH, CD])
        wo = view("A", 32, [NH, D])
        wqT1 = view("A", 0, [NH, D])
        wkT1 = view("A", 16, [NKV, CD])
        wvT1 = view("A", 20, [NKV, CD])
        wo1 = view("A", 24, [NH, D])
        wvo = view("C", 0, [NH, D])
        k_gain = view("C", 16, [TOK])
        k_sq = view("C", 20, [TOK])
        k_rn = view("C", 24, [TOK])
        k_T = view("C", 28, [TOK])
        wqk = view("C", 16, [NH, KH, CD])
        q_T = view("C", 32, [TOK])
        q_sq = view("C", 36, [TOK])
        sm_t = [view("C", 40 + 4 * i, [NT, S]) for i in range(2)]
        sm_e = [view("C", 42 + 4 * i, [NT, S]) for i in range(2)]
        p_T = view("C", 48, [4, 128])
        o_T = view("C", 50, [TOK])
        mask_add = view("C", 54, [NT, S])
        mask_f = view("C", 56, [NT, S])
        mask_u8 = view("C", 58, [NT, S], U8)
        f_fc = view("B", 0, [KH, 2 * HID])
        f_proj = view("B", 16, [2 * HB, D])
        f_neg = [view("C", 2 * i, [HALF]) for i in range(2)]
        f_leaky = [view("C", 4 + 2 * i, [HALF]) for i in range(2)]
        f_act = [view("C", 8 + 2 * i, [HALF]) for i in range(4)]
        f_router = view("C", 60, [KH, 2])
        a_wqkv = view("B", 32, [KH, 3 * D])
        a_wout = view("B", 38, [KH, D])
        a_bias = view("A", 40, [NH, S])
        a_bv = view("A", 44, [D])
        a_bo = view("A", 45, [D])
        a_q = view("C", 0, [KH, TOK])
        a_k = view("C", 8, [KH, TOK])
        a_v = view("C", 16, [NT, D])
        a_qm = [view("C", 24 + 4 * i, [TOK]) for i in range(2)]
        a_o = view("C", 0, [NT, D])
        a_oT = view("C", 8, [KH, TOK])
        t_w = [view("B", 8 * i, [2048]) for i in range(3)]
        t_wq = [view("B", kb, [2048], BF16) for kb in (24, 28, 40)]
        t_gate_q = t_wq[0].rearrange("p (k n) -> p k n", k=KH)
        t_up_q = t_wq[1].rearrange("p (k n) -> p k n", k=KH)
        t_down_q = t_wq[2].rearrange("p (k n) -> p k n", k=HB)
        t_xr = view("C", 0, [NT, D])
        t_xq = view("C", 8, [NT, D], BF16)
        t_xqT = view("C", 12, [KH, TOK], BF16)
        t_gate = [view("C", 16 + 4 * i, [HID]) for i in range(2)]
        t_h = [view("C", 24 + 4 * i, [HID]) for i in range(2)]
        t_hq = [view("C", 32 + 2 * i, [HID], BF16) for i in range(2)]
        t_hqT = view("C", 36, [HB, 128], BF16)
        t_r = view("C", 40, [HID])

        def tiles2(a):
            return ps[:, a, :].rearrange("p (t n) -> p t n", t=2)

        def pair(a):
            return ps[:, a:a + 2, :].rearrange("p a n -> p (a n)")

        def spread(col8):
            return col8.unsqueeze(2).to_broadcast([128, NT, S])

        def head_order(layer):
            order = [(("wvo", i, 0), "dve") for i in range(NH // 2)]
            if layer == 1:
                order += [(("wqk", i, 0), "act") for i in range(NH // 2)]
            for i in range(NH + 2):
                if i < NH:
                    order += [(("q", i, c), "act") for c in range(2)]
                    if layer == 0:
                        order += [(("k", i, c), "act") for c in range(2)]
                        order += [(("ss", i, c), "act") for c in range(2)]
                        order += [(("qn", i, 0), "act")]
                if 1 <= i <= NH:
                    order += [(("o", i - 1, r), "dve") for r in range(2)]
            return order

        TURNS = [work_turns(head_order(0)), work_turns(head_order(1))]
        NTURNS = [len(t) for t in TURNS]

        block = ctx.enter_context(nc.Block())

        @block.sync
        def _(sp):
            def load(dst, src, name):
                sp.dma_start(dst, src).then_inc(sem(name), 16)

            for t in range(NT):
                load(x[:, t, :], io["x"][:, t, :], "ld_x")
            for k in range(KH):
                load(m_win[:, k, :], io["m_win"][:, k, :], "ld_m")
            for dst, name in ((ident, "ident"), (ones, "ones"), (identb, "identb"), (sel_c, "sel_c"), (sel_b, "sel_b"),
                              (a_log, "a_log"), (mpar, "mpar"), (head_mask, "head_mask")):
                load(dst[:], io[name], "ld_const")
            load(small[:, 3:5], io["g"], "ld_const")
            load(qkb[:, :], io["a_bqk"], "ld_const")
            load(m_wdt, io["m_wdt"], "ld_m")
            load(m_wout, io["m_wout"], "ld_m")
            load(wvT, io["x0_wvT"], "ld_x0")
            load(wo, io["x0_wo"], "ld_x0")
            load(wq, io["x0_wq"], "ld_x0")
            load(wk, io["x0_wk"], "ld_x0")
            load(ctxT[:, :], io["ctxT"], "ld_x0")
            load(ctxn[:, :, :], io["ctxn"], "ld_x0")
            for k in range(-1, NK):
                sp.wait_ge(sem("m_parts"), k + 2)
                if k < 0:
                    for part in range(3):
                        for a in range(2):
                            load(m_sb[32 * part:32 * part + 32, a, :], m_part[part][32 * a:32 * a + 32, :], "ld_sb")
                    sp.wait_ge(sem("ld_sb"), 96)
                else:
                    if k > 0:
                        sp.wait_ge(sem("m_c"), DST * k)
                    for part in range(3):
                        for a in range(4):
                            load(m_sc[32 * part:32 * part + 32, a, :], m_part[part][32 * a:32 * a + 32, :], "ld_sc")
            sp.wait_ge(sem("x_done"), 1)
            for name, dst in (("f_router", f_router), ("f_fc", f_fc), ("f_proj", f_proj)):
                load(dst, io[name], "ld_f")
            load(a_wqkv, io["a_wqkv"], "ld_a")
            load(a_wout, io["a_wout"], "ld_a")
            sp.wait_ge(sem("x_done"), 2)
            load(a_bias, io["a_bias"], "ld_a")
            load(a_bv, io["a_bv"].partition_broadcast(128), "ld_a")
            load(a_bo, io["a_bo"].partition_broadcast(128), "ld_a")
            for name, dst in (("x1_wvT", wvT1), ("x1_wo", wo1), ("x1_wqT", wqT1), ("x1_wkT", wkT1)):
                load(dst, io[name], "ld_x1")
            sp.wait_ge(sem("x_done"), 3)
            for i, name in enumerate(("t_gate", "t_up", "t_down")):
                load(t_w[i], io[name], "ld_t")
            sp.wait_ge(sem("x_done"), 4)
            for s in range(2):
                m = io["mask"].rearrange("(p s) k -> s p k", s=2)[s]
                load(mask_u8[64 * s:64 * s + 64, :, :], m.partition_broadcast(64), "ld_x1m")
            for t in range(NT):
                sp.wait_ge(sem("y_done"), t + 1)
                sp.dma_start(out[:, t, :], x[:, t, :]).then_inc(sem("st_out"), 16)
            sp.wait_ge(sem("st_out"), 16 * NT)

        @block.gpsimd
        def _(pool):
            step = Counted(sem("pool_step"))
            for h in range(NH):
                pool.wait_ge(sem("a_qk"), 8)
                if h >= 2:
                    pool.wait_ge(sem("a_s"), h - 1)
                pool.tensor_scalar(a_qm[h % 2], a_q[:, h // 8, :], head_mask[:, h % 8:h % 8 + 1], None,
                                   ALU.mult).then_inc(sem("a_qm"), 1)
            pool.wait_ge(sem("t_ws"), 1)
            for i in range(3):
                step.on(pool.tensor_scalar(t_w[i], t_w[i], small[:, 19 + i:20 + i], 1.0, ALU.mult, ALU.min))
                pool.wait_ge(step.sem, step.n)
                step.on(pool.tensor_scalar(t_w[i], t_w[i], -1.0, MAGIC, ALU.max, ALU.add))
                pool.wait_ge(step.sem, step.n)
                pool.tensor_scalar(t_wq[i], t_w[i], MAGIC, None, ALU.subtract).then_inc(sem("t_wq"), 1)

        @block.scalar
        def _(act):
            step = Counted(sem("act_step"))

            def after(ins):
                step.on(ins)
                act.wait_ge(step.sem, step.n)

            def norm_rows(ln, transposed=True):
                act.wait_ge(sem("ln_var"), ln + 1)
                after(act.activation(rstd[:, :], mv[:, :, 1], ACT.Ln, bias=eps_col))
                act.activation(rstd[:, :], rstd[:, :], ACT.Exp, scale=-0.5).then_inc(sem("ln_rstd"), 1)
                if transposed:
                    for g in range(4):
                        act.wait_ge(sem("ln_tr"), 4 * ln + g + 1)
                        act.activation(xnT[:, :, 256 * g:256 * g + 256], tiles2(g), ACT.Copy)\
                            .then_inc(sem("ln_T"), 1)

            act.wait_ge(sem("ready"), 1)
            norm_rows(0)
            act.wait_ge(sem("ld_const"), 160)
            act.activation(a_log[:, :, :], a_log[:, :, :], ACT.Exp).then_inc(sem("m_aexp"), 1)
            def split(bank, rows):
                p0, p1 = m_part[0][0:rows], m_part[1][0:rows]
                act.activation(p0, pair(bank)[0:rows], ACT.Copy).then_inc(sem("m_p0"), 1)

            for k in range(NK):
                base = 6 + 4 * (k - 1) if k else 0
                if k == 0:
                    act.wait_ge(sem("m_proj"), 1)
                    act.activation(m_dtl, pair(0), ACT.Copy).then_inc(sem("m_dtl"), 1)
                    act.wait_ge(sem("m_proj"), 2)
                    split(2, 64)
                    act.wait_ge(sem("m_r1"), 1)
                    act.activation(m_part[1][0:64], m_rest[0:64], ACT.Copy).then_inc(sem("m_p1"), 1)
                    base = 2
                    act.wait_ge(sem("ld_sb"), 96)
                else:
                    act.wait_ge(sem("ld_sc"), 192 * k)
                act.wait_ge(sem("m_proj"), base + 1)
                split(4, 128)
                act.wait_ge(sem("m_r1"), k + 2)
                act.activation(m_part[1], m_rest, ACT.Copy).then_inc(sem("m_p1"), 1)
                act.wait_ge(sem("m_proj"), base + 3)
                act.activation(m_zs, pair(2), ACT.Silu).then_inc(sem("m_zs"), 1)
                act.wait_ge(sem("m_conv"), k + 1)
                act.activation(m_u, m_h[0], ACT.Silu, bias=mpar[:, k, 4:5]).then_inc(sem("m_u"), 1)
                act.wait_ge(sem("m_proj"), base + 4)
                act.wait_ge(sem("m_b2"), 1)
                act.activation(m_dbu[0], pair(4), ACT.Identity, bias=mpar[:, k, 7:8]).then_inc(sem("m_dtx"), 1)
                after(act.activation(m_dbu[1], pair(4), ACT.Abs, bias=mpar[:, k, 7:8]))
                after(act.activation(m_hc[0], m_dbu[1], ACT.Exp, scale=-1.0))
                act.activation(m_hc[1], m_hc[0], ACT.Ln, bias=one_col).then_inc(sem("m_ln"), 1)
                act.wait_ge(sem("m_delta"), k + 1)
                for n in range(DST):
                    u = DST * k + n
                    if u >= 2:
                        act.wait_ge(sem("m_scan"), u - 1)
                    act.activation(m_da[n % 2][:, :, 1:S], m_delta[:, :, 1:S], ACT.Exp,
                                   scale=a_log[:, k, n:n + 1]).then_inc(sem("m_da"), 1)

            def cross(layer):
                turns, tag = TURNS[layer], f"x{layer}"
                filled, freed = sem(tag + "_filled"), sem(tag + "_free_act")

                def bank(job):
                    w = turns[job][0]
                    act.wait_ge(filled, w + 1)
                    return ps[:, 6 + w % 2, :]

                if layer == 1:
                    for i in range(NH // 2):
                        b = bank(("wqk", i, 0))
                        act.activation(wqk[:, 2 * i:2 * i + 2].rearrange("p a b c -> p (a b c)"), b,
                                       ACT.Copy).then_inc(freed, 1)

                def exps(i):
                    act.wait_ge(sem(tag + "_shift"), i + 1)
                    act.activation(sm_e[0], sm_t[0], ACT.Exp).then_inc(sem(tag + "_exp"), 1)

                for i in range(NH + 1):
                    if i < NH:
                        for c in range(2):
                            cs = slice(c * HALF, c * HALF + HALF)
                            b = bank(("q", i, c))
                            if layer == 0:
                                act.activation(q_sq[:, cs], b, ACT.Square)
                            act.activation(q_T[:, cs], b, ACT.Copy).then_inc(freed, 1)
                            if c == 0 and i >= 1:
                                exps(i - 1)
                    else:
                        exps(i - 1)
                    if i < NH and layer == 0:
                        for c in range(2):
                            cs = slice(c * HALF, c * HALF + HALF)
                            b = bank(("k", i, c))
                            act.activation(k_sq[:, cs], b, ACT.Square)
                            act.activation(k_gain[:, cs], b, ACT.Copy, scale=g_col).then_inc(freed, 1)
                    if i >= 1:
                        act.wait_ge(sem(tag + "_tr"), i)
                        act.activation(p_T, ps[:, 5, :].rearrange("p (a b) -> p a b", a=4), ACT.Copy)\
                            .then_inc(sem(tag + "_pT"), 1)
                    if i < NH and layer == 0:
                        for c in range(2):
                            cs = slice(c * HALF, c * HALF + HALF)
                            b = bank(("ss", i, c))
                            act.activation(k_rn[:, cs], b, ACT.Ln, scale=1.0 / HD, bias=eps_col).then_inc(freed, 1)
                            act.wait_ge(freed, turns[("ss", i, c)][2])
                            act.activation(k_rn[:, cs], k_rn[:, cs], ACT.Exp, scale=-0.5)\
                                .then_inc(sem("x0_rk"), 1)
                        b = bank(("qn", i, 0))
                        act.activation(small[:, 40:48], b[:, 0:8], ACT.Ln, scale=1.0 / HD, bias=eps_col)\
                            .then_inc(freed, 1)
                        act.wait_ge(freed, turns[("qn", i, 0)][2])
                        act.activation(small[:, 48:56], small[:, 40:48], ACT.Exp, scale=-0.5)\
                            .then_inc(sem("x0_rq"), 1)

            norm_rows(1)
            act.wait_ge(sem("x0_g"), 1)
            cross(0)
            norm_rows(2)
            act.wait_ge(sem("f_ld"), 1)
            act.activation(small[:, 24:32], small[:, 16:24], ACT.Exp, scale=-1.0).then_inc(sem("f_e"), 1)
            for n in range(4 * HB):
                act.wait_ge(sem("f_leaky"), n + 1)
                if n >= 4:
                    act.wait_ge(sem("f_pr"), n - 3)
                act.activation(f_act[n % 4], f_leaky[n % 2], ACT.Square).then_inc(sem("f_act"), 1)
            norm_rows(3)
            for n in range(8):
                act.wait_ge(sem("a_proj"), n + 1)
                dst = (a_q if n < 4 else a_k)[:, n // 2 % 2, HALF * (n % 2):HALF * (n % 2) + HALF]
                act.activation(dst, ps[:, 4 + n % 4, :], ACT.Identity, bias=qkb[:, n // 2:n // 2 + 1])\
                    .then_inc(sem("a_qk"), 1)
            for i in range(NH + 2):
                if i < NH:
                    act.wait_ge(sem("a_shift"), i + 1)
                    act.activation(sm_e[i % 2], sm_t[i % 2], ACT.Exp).then_inc(sem("a_exp"), 1)
                if i >= 2:
                    act.wait_ge(sem("a_tr"), i - 1)
                    act.activation(p_T, ps[:, 5, :].rearrange("p (a b) -> p a b", a=4), ACT.Copy)\
                        .then_inc(sem("a_pT"), 1)
            for g in range(4):
                act.wait_ge(sem("a_otr"), g + 1)
                act.activation(a_oT[:, :, 256 * g:256 * g + 256], tiles2(4 + g), ACT.Copy)\
                    .then_inc(sem("a_oT"), 1)
            norm_rows(4)
            cross(1)
            norm_rows(5, transposed=False)
            for g in range(2):
                act.wait_ge(sem("t_xtr"), g + 1)
                act.activation(t_xqT[:, :, HALF * g:HALF * g + HALF],
                               ps[:, 2 * g, :].bitcast(BF16).rearrange("p (k n) -> p k n", k=KH), ACT.Copy)\
                    .then_inc(sem("t_xT"), 1)
            for t in range(NT + 1):
                if t < NT:
                    act.wait_ge(sem("t_gu"), t + 1)
                    act.wait_ge(sem("t_sc"), 1)
                    if t >= 2:
                        act.wait_ge(sem("t_prod"), t - 1)
                    act.activation(t_gate[t % 2], pair(0), ACT.Silu, scale=small[:, 56 + t:57 + t])\
                        .then_inc(sem("t_gate"), 1)
                if t >= 1:
                    act.wait_ge(sem("t_htr"), t)
                    act.activation(t_hqT, ps[:, 4, :].bitcast(BF16).rearrange("p (k n) -> p k n", k=HB),
                                   ACT.Copy).then_inc(sem("t_hT"), 1)

        @block.tensor
        def _(pe):
            def norm_rows(ln):
                for g in range(4):
                    pe.wait_ge(sem("ln_xn"), 8 * ln + 2 * g + 2)
                    for k in range(KH):
                        for a in range(2):
                            last = pe.transpose(tiles2(g)[:, k, 128 * a:128 * a + 128],
                                                xn[:, 2 * g + a, 128 * k:128 * k + 128], ident[:, :])
                    last.then_inc(sem("ln_tr"), 1)
                pe.wait_ge(sem("ln_T"), 4 * ln + 4)

            pe.wait_ge(sem("ld_const"), 160)
            norm_rows(0)
            pe.wait_ge(sem("ld_m"), 64)

            def project(bank, lhs, rows=128, rhs=None, halves=KH):
                for c in range(2):
                    for k in range(halves):
                        last = pe.matmul(ps[0:rows, bank + c, :], lhs(k),
                                         (rhs if rhs is not None else xnT[:, k, :])[:, c * HALF:c * HALF + HALF],
                                         start=(k == 0), stop=(k == halves - 1))
                last.then_inc(sem("m_proj"), 1)

            for kk in range(NK):
                if kk == 0:
                    project(0, lambda k: m_win[:, k, M_DT:M_COLS])
                    project(2, lambda k: m_win[:, k, M_B:M_C], 64)
                else:
                    pe.wait_ge(sem("m_scan"), DST * kk)
                    pe.wait_ge(sem("m_hc"), DST * kk)
                project(4, lambda k: m_win[:, k, M_C + 128 * kk:M_C + 128 * kk + 128])
                if kk == 0:
                    pe.wait_ge(sem("m_dtl"), 1)
                project(0, lambda k: m_win[:, k, M_X + 128 * kk:M_X + 128 * kk + 128])
                pe.wait_ge(sem("m_r1"), 1)
                project(2, lambda k: m_win[:, k, 128 * kk:128 * kk + 128])
                pe.wait_ge(sem("m_r1"), kk + 2)
                project(4, lambda k: m_wdt[:, 128 * kk:128 * kk + 128], 128, m_dtl, 1)
                pe.wait_ge(sem("ld_sb"), 96)
                pe.wait_ge(sem("ld_sc"), 192 * (kk + 1))

                def put_b(n):
                    u = DST * kk + n
                    if n >= 2:
                        pe.wait_ge(sem("m_dbu"), u - 1)
                    r = u % 32
                    for c in range(2):
                        last = pe.matmul(ps[:, 2 * (n % 2) + c, :], sel_b[:, r, :],
                                         m_sb[:, u // 32, c * HALF:c * HALF + HALF], start=True, stop=True)
                    last.then_inc(sem("m_b"), 1)

                pe.wait_ge(sem("m_conv"), kk + 1)
                pe.wait_ge(sem("m_zs"), kk + 1)
                put_b(0)
                pe.wait_ge(sem("m_ln"), kk + 1)
                for n in range(DST + 1):
                    u = DST * kk + n
                    if n + 1 < DST:
                        put_b(n + 1)
                    if n < DST:
                        if n >= 1:
                            pe.wait_ge(sem("m_hc"), u)
                        for c in range(2):
                            last = pe.matmul(ps[:, 4 + c, :], sel_c[:, n % 4, :],
                                             m_sc[:, n // 4, c * HALF:c * HALF + HALF], start=True, stop=True)
                        last.then_inc(sem("m_c"), 1)
                    if n >= 1:
                        pe.wait_ge(sem("m_hc"), u)
                        if n == 1 and kk >= 1:
                            pe.wait_ge(sem("m_yd"), kk)
                        for c in range(2):
                            last = pe.matmul(ps[:, 6 + c, :], ident[:, :],
                                             m_hc[(n - 1) % 2][:, c * HALF:c * HALF + HALF],
                                             start=(n == 1), stop=(n == DST))
                        last.then_inc(sem("m_y"), 1)
            pe.wait_ge(sem("m_yg"), NK)
            for t in range(NT):
                for k in range(NK):
                    last = pe.matmul(tiles2(t // 2)[:, t % 2, :], m_yg[:, k, 128 * t:128 * t + 128], m_wout[:, k, :],
                                     start=(k == 0), stop=(k == NK - 1))
                last.then_inc(sem("m_out"), 1)

            def cross(layer):
                turns, tag = TURNS[layer], f"x{layer}"
                by_turn = {w: (by, n) for w, by, n in turns.values()}
                pe.wait_ge(sem("ld_" + tag), 96 if layer == 0 else 64)

                def bank(job):
                    w = turns[job][0]
                    if w >= 2:
                        by, n = by_turn[w - 2]
                        pe.wait_ge(sem(f"{tag}_free_{by}"), n)
                    return ps[:, 6 + w % 2, :]

                filled = sem(tag + "_filled")
                wv_h, wo_h = (wvT, wo) if layer == 0 else (wvT1, wo1)
                for i in range(NH // 2):
                    b = bank(("wvo", i, 0))
                    for a in range(2):
                        h = 2 * i + a
                        last = pe.matmul(b[:, 256 * a:256 * a + 256], wv_h[:, h if layer == 0 else h // 2, :],
                                         wo_h[:, h, :], start=True, stop=True)
                    last.then_inc(filled, 1)
                if layer == 1:
                    for i in range(NH // 2):
                        b = bank(("wqk", i, 0))
                        for a in range(2):
                            for k in range(KH):
                                c = (2 * a + k) * 128
                                last = pe.matmul(b[:, c:c + 128], wqT1[:, 2 * i + a, 128 * k:128 * k + 128],
                                                 wkT1[:, i, :], start=True, stop=True)
                        last.then_inc(filled, 1)

                def queries(i):
                    for c in range(2):
                        b = bank(("q", i, c))
                        for k in range(KH):
                            w = wq[:, k, HD * i:HD * i + HD] if layer == 0 else wqk[:, i, k, :]
                            last = pe.matmul(b, w, xnT[:, k, c * HALF:c * HALF + HALF],
                                             start=(k == 0), stop=(k == KH - 1))
                        last.then_inc(filled, 1)

                def keys(i):
                    for c in range(2):
                        b = bank(("k", i, c))
                        pe.matmul(b, wk[:, HD * i:HD * i + HD], ctxT[:, c * HALF:c * HALF + HALF],
                                  start=True, stop=True).then_inc(filled, 1)

                def norms(i):
                    for c in range(2):
                        b = bank(("ss", i, c))
                        pe.wait_ge(sem("x0_free_act"), turns[("k", i, c)][2])
                        pe.matmul(b, ones[:, :], k_sq[:, c * HALF:c * HALF + HALF],
                                  start=True, stop=True).then_inc(filled, 1)
                    b = bank(("qn", i, 0))
                    for t in range(NT):
                        last = pe.matmul(b[:, t:t + 1], q_sq[:, 128 * t:128 * t + 128], ones[:, 0:1],
                                         start=True, stop=True)
                    last.then_inc(filled, 1)

                def scores(i):
                    pe.wait_ge(sem(tag + "_free_act"), turns[("q", i, 1)][2])
                    if layer == 0:
                        pe.wait_ge(sem("x0_kT"), 2 * i + 2)
                    if i >= 1:
                        pe.wait_ge(sem(tag + "_t"), i)
                    kk = k_T if layer == 0 else ctxT
                    for b in range(B):
                        last = pe.matmul(ps[64 * (b % 2):64 * (b % 2) + 64, 4, S * (b // 2):S * (b // 2) + S],
                                         q_T[:, S * b:S * b + S], kk[:, S * b:S * b + S], start=True, stop=True)
                    last.then_inc(sem(tag + "_s"), 1)

                def turn_probs(i):
                    pe.wait_ge(sem(tag + "_p"), i + 1)
                    if i >= 1:
                        pe.wait_ge(sem(tag + "_pT"), i)
                    for j in range(4):
                        last = pe.transpose(ps[:, 5, 128 * j:128 * j + 128],
                                            sm_t[1][:, 2 * j:2 * j + 2, :].rearrange("p a b -> p (a b)"), ident[:, :])
                    last.then_inc(sem(tag + "_tr"), 1)

                def context(i):
                    pe.wait_ge(sem(tag + "_pT"), i + 1)
                    for r in range(2):
                        b = bank(("o", i, r))
                        for j in range(4):
                            for s in range(2):
                                c = (2 * j + s) * S
                                last = pe.matmul(b[:, c:c + S], ctxn[64 * r:64 * r + 64, 2 * j + s, :],
                                                 p_T[64 * r:64 * r + 64, j, 64 * s:64 * s + 64],
                                                 start=True, stop=True)
                        last.then_inc(filled, 1)

                def project_out(i):
                    pe.wait_ge(sem(tag + "_free_dve"), turns[("o", i, 1)][2])
                    for t in range(NT):
                        last = pe.matmul(tiles2(t // 2)[:, t % 2, :], o_T[:, 128 * t:128 * t + 128], wvo[:, i, :],
                                         start=(i == 0 and t % 2 == 0), stop=(i == NH - 1),
                                         skip_group_check=True)
                    last.then_inc(sem(tag + "_out"), 1)

                for i in range(NH + 2):
                    if i < NH:
                        queries(i)
                        if layer == 0:
                            keys(i)
                    if i >= 2:
                        project_out(i - 2)
                    if 1 <= i <= NH:
                        turn_probs(i - 1)
                    if i < NH and layer == 0:
                        norms(i)
                    if 1 <= i <= NH and layer == 0:
                        context(i - 1)
                    if i < NH:
                        scores(i)
                    if 1 <= i <= NH and layer == 1:
                        context(i - 1)

            norm_rows(1)
            cross(0)
            norm_rows(2)
            pe.wait_ge(sem("ld_f"), 48)
            for t in range(NT):
                for k in range(KH):
                    last = pe.matmul(ps[:, 7, 2 * t:2 * t + 2], xnT[:, k, 128 * t:128 * t + 128], f_router[:, k, :],
                                     start=(k == 0), stop=(k == KH - 1))
            last.then_inc(sem("f_logit"), 1)

            def hidden(n):
                c, e, hb = n // (2 * HB), n // HB % 2, n % HB
                if n == 3:
                    pe.wait_ge(sem("f_diff"), 1)
                if n >= 4:
                    pe.wait_ge(sem("f_leaky"), n - 3)
                for k in range(KH):
                    last = pe.matmul(ps[:, 4 + n % 4, :], f_fc[:, k, HID * e + 128 * hb:HID * e + 128 * hb + 128],
                                     xnT[:, k, c * HALF:c * HALF + HALF], start=(k == 0), stop=(k == KH - 1))
                last.then_inc(sem("f_h"), 1)

            def expert_out(n):
                e, hb = n // HB % 2, n % HB
                pe.wait_ge(sem("f_act"), n + 1)
                if n >= 2 * HB and hb == 0:
                    pe.wait_ge(sem("f_x"), n // HB - 1)
                for t in range(4):
                    last = pe.matmul(tiles2(2 * e + t // 2)[:, t % 2, :], f_act[n % 4][:, 128 * t:128 * t + 128],
                                     f_proj[:, HB * e + hb, :], start=(hb == 0 and t % 2 == 0),
                                     stop=(hb == HB - 1), skip_group_check=True)
                last.then_inc(sem("f_pr"), 1)

            for n in range(4 * HB + 2):
                if n < 4 * HB:
                    hidden(n)
                if n >= 2:
                    expert_out(n - 2)
            norm_rows(3)
            pe.wait_ge(sem("ld_a"), 80)
            for n in range(8):
                if n >= 4:
                    pe.wait_ge(sem("a_qk"), n - 3)
                for k in range(KH):
                    last = pe.matmul(ps[:, 4 + n % 4, :], a_wqkv[:, k, 128 * (n // 2):128 * (n // 2) + 128],
                                     xnT[:, k, HALF * (n % 2):HALF * (n % 2) + HALF],
                                     start=(k == 0), stop=(k == KH - 1))
                last.then_inc(sem("a_proj"), 1)
            for j in range(4):
                for s in range(2):
                    for r in range(2):
                        b = 4 * j + 2 * r + s
                        for k in range(KH):
                            last = pe.matmul(tiles2(j)[64 * r:64 * r + 64, s, :], xnT[:, k, S * b:S * b + S],
                                             a_wqkv[:, k, 2 * D:3 * D], start=(k == 0), stop=(k == KH - 1))
                last.then_inc(sem("a_vproj"), 1)
            for i in range(NH + 3):
                if i < NH:
                    pe.wait_ge(sem("a_qm"), i + 1)
                    pe.wait_ge(sem("a_qk"), 8)
                    if i >= 2:
                        pe.wait_ge(sem("a_t"), i - 1)
                    for b in range(B):
                        last = pe.matmul(ps[64 * (b % 2):64 * (b % 2) + 64, 4 + 2 * (i % 2),
                                            S * (b // 2):S * (b // 2) + S],
                                         a_qm[i % 2][:, S * b:S * b + S], a_k[:, i // 8, S * b:S * b + S],
                                         start=True, stop=True)
                    last.then_inc(sem("a_s"), 1)
                if i >= 3:
                    h = i - 3
                    pe.wait_ge(sem("a_pT"), h + 1)
                    pe.wait_ge(sem("a_v"), 4)
                    for r in range(2):
                        for j in range(4):
                            for s in range(2):
                                last = pe.matmul(ps[64 * s:64 * s + 64, 2 * r + j // 2,
                                                    256 * (j % 2) + HDS * h:256 * (j % 2) + HDS * h + HDS],
                                                 p_T[64 * r:64 * r + 64, j, 64 * s:64 * s + 64],
                                                 a_v[64 * r:64 * r + 64, 2 * j + s, HDS * h:HDS * h + HDS],
                                                 start=True, stop=True)
                    last.then_inc(sem("a_ctx"), 1)
                if 2 <= i < NH + 2:
                    h = i - 2
                    pe.wait_ge(sem("a_p"), h + 1)
                    if h >= 1:
                        pe.wait_ge(sem("a_pT"), h)
                    for j in range(4):
                        last = pe.transpose(ps[:, 5, 128 * j:128 * j + 128],
                                            sm_e[h % 2][:, 2 * j:2 * j + 2, :].rearrange("p a b -> p (a b)"),
                                            ident[:, :])
                    last.then_inc(sem("a_tr"), 1)
            for g in range(4):
                pe.wait_ge(sem("a_o"), 4)
                for k in range(KH):
                    for a in range(2):
                        last = pe.transpose(tiles2(4 + g)[:, k, 128 * a:128 * a + 128],
                                            a_o[:, 2 * g + a, 128 * k:128 * k + 128], ident[:, :])
                last.then_inc(sem("a_otr"), 1)
            for t in range(NT):
                pe.wait_ge(sem("a_oT"), t // 2 + 1)
                for k in range(KH):
                    last = pe.matmul(tiles2(t // 2)[:, t % 2, :], a_oT[:, k, 128 * t:128 * t + 128], a_wout[:, k, :],
                                     start=(k == 0), stop=(k == KH - 1))
                last.then_inc(sem("a_out"), 1)
            norm_rows(4)
            pe.wait_ge(sem("t_abs"), 3)
            pe.matmul(ps[:, 4, 0:3], ones[:, :], small[:, 8:11], start=True, stop=True).then_inc(sem("t_sum"), 1)
            pe.wait_ge(sem("t_ws"), 1)
            cross(1)
            for g in range(2):
                pe.wait_ge(sem("t_xq"), 1)
                xt = ps[:, 2 * g, :].bitcast(BF16).rearrange("p (k n) -> p k n", k=KH)
                for k in range(KH):
                    for t in range(4):
                        last = pe.transpose(xt[:, k, 128 * t:128 * t + 128],
                                            t_xq[:, 4 * g + t, 128 * k:128 * k + 128], identb[:, :])
                last.then_inc(sem("t_xtr"), 1)
            pe.wait_ge(sem("t_xT"), 2)
            pe.wait_ge(sem("t_wq"), 3)
            for t in range(NT + 1):
                if t < NT:
                    if t >= 1:
                        pe.wait_ge(sem("t_gate"), t)
                        pe.wait_ge(sem("t_prod"), t)
                    for o, w in ((0, t_gate_q), (2, t_up_q)):
                        for c in range(2):
                            for k in range(KH):
                                last = pe.matmul(ps[:, o + c, :], t_xqT[:, k, 128 * t:128 * t + 128],
                                                 w[:, k, 512 * c:512 * c + 512], start=(k == 0), stop=(k == KH - 1))
                    last.then_inc(sem("t_gu"), 1)
                if t >= 1:
                    pe.wait_ge(sem("t_hq"), t)
                    ht = ps[:, 4, :].bitcast(BF16)
                    for k in range(HB):
                        last = pe.transpose(ht[:, 128 * k:128 * k + 128], t_hq[(t - 1) % 2][:, 128 * k:128 * k + 128],
                                            identb[:, :])
                    last.then_inc(sem("t_htr"), 1)
                    pe.wait_ge(sem("t_hT"), t)
                    if t >= 3:
                        pe.wait_ge(sem("y_done"), t - 2)
                    for k in range(HB):
                        last = pe.matmul(ps[:, 5 + (t - 1) % 2, 0:D], t_hqT[:, k, :], t_down_q[:, k, :],
                                         start=(k == 0), stop=(k == HB - 1))
                    last.then_inc(sem("t_dn"), 1)

        @block.vector
        def _(dve):
            step = Counted(sem("dve_step"))

            def after(ins):
                step.on(ins)
                dve.wait_ge(step.sem, step.n)

            def norm_rows(ln):
                for t in range(NT):
                    if ln == 0:
                        dve.wait_ge(sem("ld_x"), 16 * NT)
                    last = dve.bn_stats(stats[:, t, :], x[:, t, :])
                after(last)
                for t in range(NT):
                    last = dve.bn_aggr(mv[:, t, :], stats[:, t, :])
                last.then_inc(sem("ln_var"), 1)
                dve.wait_ge(sem("ln_rstd"), ln + 1)
                for t in range(NT):
                    dve.tensor_scalar(xn[:, t, :], x[:, t, :], mv[:, t, 0:1], rstd[:, t:t + 1],
                                      ALU.subtract, ALU.mult).then_inc(sem("ln_xn"), 1)

            dve.memset(eps_col, EPS)
            dve.memset(one_col, 1.0)
            dve.memset(zero_col, 0.0).then_inc(sem("ready"), 1)
            norm_rows(0)
            for i in range(2):
                after(dve.memset(m_da[i][:, :, 0:1], 0.0))
            dve.wait_ge(sem("ld_const"), 160)
            dve.tensor_scalar(mpar[:, :, 7:8], mpar[:, :, 6:7], 2.0, None, ALU.mult).then_inc(sem("m_b2"), 1)
            dve.wait_ge(sem("m_aexp"), 1)
            after(dve.tensor_scalar(a_log[:, :, :], a_log[:, :, :], -1.0, None, ALU.mult))

            def split(bank, rows, count):
                rest = m_rest[0:rows]
                dve.wait_ge(sem("m_p0"), count)
                dve.tensor_tensor(rest, pair(bank)[0:rows], m_part[0][0:rows], ALU.subtract)\
                    .then_inc(sem("m_r1"), 1)
                dve.wait_ge(sem("m_p1"), count)
                dve.tensor_tensor(m_part[2][0:rows], rest, m_part[1][0:rows], ALU.subtract)\
                    .then_inc(sem("m_parts"), 1)

            for k in range(NK):
                base = 2 if k == 0 else 6 + 4 * (k - 1)
                if k == 0:
                    split(2, 64, 1)
                    dve.wait_ge(sem("ld_sb"), 96)
                else:
                    dve.wait_ge(sem("ld_sc"), 192 * k)
                split(4, 128, k + 2)
                dve.wait_ge(sem("m_proj"), base + 2)
                raw = pair(0).rearrange("p (b t) -> p b t", t=S)
                acc = m_h[0].rearrange("p (b t) -> p b t", t=S)
                after(dve.tensor_scalar(m_h[0], pair(0), mpar[:, k, DCONV - 1:DCONV], None, ALU.mult))
                for lag in range(1, DCONV):
                    ins = dve.scalar_tensor_tensor(out=acc[:, :, lag:], in0=raw[:, :, :S - lag],
                                                   scalar=mpar[:, k, DCONV - 1 - lag:DCONV - lag],
                                                   in1=acc[:, :, lag:], op0=ALU.mult, op1=ALU.add)
                    if lag < DCONV - 1:
                        after(ins)
                ins.then_inc(sem("m_conv"), 1)
                dve.wait_ge(sem("m_ln"), k + 1)
                e, ln1 = m_hc[0], m_hc[1]
                after(dve.tensor_scalar(m_h[1], e, 1.0 / 3.0, -0.5, ALU.mult, ALU.add))
                after(dve.tensor_tensor(m_h[1], m_h[1], e, ALU.mult))
                after(dve.scalar_tensor_tensor(out=m_h[1], in0=m_h[1], scalar=1.0, in1=e, op0=ALU.add, op1=ALU.mult))
                dve.wait_ge(sem("m_u"), k + 1)
                after(dve.tensor_scalar(m_dbu[1], e, LOG1P_SPLIT, None, ALU.is_lt))
                after(dve.copy_predicated(ln1, m_dbu[1].bitcast(mybir.dt.uint32), m_h[1]))
                after(dve.scalar_tensor_tensor(out=m_delta.rearrange("p b t -> p (b t)"), in0=m_dbu[0], scalar=0.0,
                                               in1=ln1, op0=ALU.max, op1=ALU.add))
                dve.tensor_tensor(m_du, m_delta.rearrange("p b t -> p (b t)"), m_u, ALU.mult)\
                    .then_inc(sem("m_delta"), 1)
                dve.wait_ge(sem("m_delta"), k + 1)
                for n in range(DST):
                    u = DST * k + n
                    dve.wait_ge(sem("m_b"), u + 1)
                    dve.tensor_tensor(m_dbu[n % 2], pair(2 * (n % 2)), m_du, ALU.mult).then_inc(sem("m_dbu"), 1)
                    dve.wait_ge(sem("m_dbu"), u + 1)
                    dve.wait_ge(sem("m_da"), u + 1)
                    dve.tensor_tensor_scan(m_h[n % 2], m_da[n % 2].rearrange("p b t -> p (b t)"), m_dbu[n % 2], 0.0,
                                           ALU.mult, ALU.add).then_inc(sem("m_scan"), 1)
                    dve.wait_ge(sem("m_scan"), u + 1)
                    dve.wait_ge(sem("m_c"), u + 1)
                    if u >= 2:
                        dve.wait_ge(sem("m_y"), u - 1)
                    dve.tensor_tensor(m_hc[n % 2], pair(4), m_h[n % 2], ALU.mult).then_inc(sem("m_hc"), 1)
                dve.wait_ge(sem("m_y"), DST * (k + 1))
                dve.scalar_tensor_tensor(out=m_yg[:, k, :], in0=m_u, scalar=mpar[:, k, 5:6], in1=pair(6),
                                         op0=ALU.mult, op1=ALU.add).then_inc(sem("m_yd"), 1)
                dve.wait_ge(sem("m_yd"), k + 1)
                dve.wait_ge(sem("m_zs"), k + 1)
                dve.tensor_tensor(m_yg[:, k, :], m_yg[:, k, :], m_zs, ALU.mult).then_inc(sem("m_yg"), 1)

            def add_tiles(ready):
                for g in range(4):
                    dve.wait_ge(ready[0], ready[1][g])
                    ins = dve.tensor_tensor(x[:, 2 * g:2 * g + 2, :], tiles2(g), x[:, 2 * g:2 * g + 2, :], ALU.add)
                ins.then_inc(sem("x_done"), 1)

            add_tiles((sem("m_out"), [2, 4, 6, 8]))
            dve.wait_ge(sem("x_done"), 1)

            def cross(layer):
                turns, tag = TURNS[layer], f"x{layer}"
                filled, freed = sem(tag + "_filled"), sem(tag + "_free_dve")

                def bank(job):
                    w = turns[job][0]
                    dve.wait_ge(filled, w + 1)
                    return ps[:, 6 + w % 2, :]

                for i in range(NH // 2):
                    b = bank(("wvo", i, 0))
                    dve.tensor_copy(wvo[:, 2 * i:2 * i + 2, :], b.rearrange("p (a n) -> p a n", a=2)).then_inc(freed, 1)
                top, den = small[:, 64:72], small[:, 72:80]

                def shift(i):
                    s = ps[:, 4, :].rearrange("p (a b) -> p a b", b=S)
                    dve.wait_ge(sem(tag + "_s"), i + 1)
                    if layer == 0:
                        dve.wait_ge(sem("x0_rq"), i + 1)
                        ins = dve.tensor_tensor(sm_t[0], s, spread(small[:, 48:56]), ALU.mult)
                    else:
                        ins = dve.scalar_tensor_tensor(out=sm_t[0], in0=s, scalar=QSCALE, in1=mask_add,
                                                       op0=ALU.mult, op1=ALU.add)
                    ins.then_inc(sem(tag + "_t"), 1)
                    dve.wait_ge(sem(tag + "_t"), i + 1)
                    after(dve.tensor_reduce(top, sm_t[0], AX.X, ALU.max))
                    dve.tensor_tensor(sm_t[0], sm_t[0], spread(top), ALU.subtract).then_inc(sem(tag + "_shift"), 1)

                def divide(i):
                    dve.wait_ge(sem(tag + "_exp"), i + 1)
                    if layer == 1:
                        after(dve.tensor_tensor(sm_e[0], sm_e[0], mask_f, ALU.mult))
                    after(dve.tensor_reduce(den, sm_e[0], AX.X, ALU.add))
                    if layer == 1:
                        after(dve.tensor_scalar(den, den, 1e-30, None, ALU.max))
                    after(dve.reciprocal(den, den))
                    dve.tensor_tensor(sm_t[1], sm_e[0], spread(den), ALU.mult).then_inc(sem(tag + "_p"), 1)

                for i in range(NH + 1):
                    if i >= 1:
                        shift(i - 1)
                        divide(i - 1)
                    if i < NH and layer == 0:
                        for c in range(2):
                            cs = slice(c * HALF, c * HALF + HALF)
                            dve.wait_ge(sem("x0_rk"), 2 * i + c + 1)
                            dve.tensor_tensor(k_T[:, cs], k_gain[:, cs], k_rn[:, cs], ALU.mult)\
                                .then_inc(sem("x0_kT"), 1)
                    if i >= 1:
                        for r in range(2):
                            b = bank(("o", i - 1, r))
                            dst = o_T.rearrange("p (j r n) -> p r j n", r=2, n=128)[:, r]
                            dve.tensor_copy(dst, b.rearrange("p (j n) -> p j n", n=128)).then_inc(freed, 1)
                add_tiles((sem(tag + "_out"), [NH] * 4))

            norm_rows(1)
            after(dve.tensor_tensor(g_col, gq_col, gk_col, ALU.mult))
            dve.tensor_scalar(g_col, g_col, QSCALE, None, ALU.mult).then_inc(sem("x0_g"), 1)
            cross(0)
            dve.wait_ge(sem("x_done"), 2)
            norm_rows(2)
            lg = ps[:, 7, 0:2 * NT].rearrange("p (t e) -> p t e", e=2)
            dlt, mag, pick = small[:, 8:16], small[:, 16:24], small[:, 32:40]
            w_e = [small[:, 80:88], small[:, 88:96]]
            dve.wait_ge(sem("f_logit"), 1)
            after(dve.tensor_copy(dlt, lg[:, :, 0]))
            dve.tensor_tensor(dlt, dlt, lg[:, :, 1], ALU.subtract).then_inc(sem("f_diff"), 1)
            dve.wait_ge(sem("f_diff"), 1)
            after(dve.tensor_scalar(mag, dlt, -1.0, None, ALU.mult))
            dve.tensor_tensor(mag, mag, dlt, ALU.max).then_inc(sem("f_ld"), 1)
            after(dve.tensor_scalar(pick, dlt, 0.0, None, ALU.is_ge))
            dve.wait_ge(sem("f_e"), 1)
            after(dve.tensor_scalar(small[:, 24:32], small[:, 24:32], 1.0, None, ALU.add))
            after(dve.reciprocal(small[:, 24:32], small[:, 24:32]))
            after(dve.tensor_tensor(w_e[0], small[:, 24:32], pick, ALU.mult))
            after(dve.tensor_tensor(w_e[1], small[:, 24:32], w_e[0], ALU.subtract))
            for n in range(4 * HB):
                h = ps[:, 4 + n % 4, :]
                dve.wait_ge(sem("f_h"), n + 1)
                after(dve.tensor_scalar(f_neg[n % 2], h, 0.0, -0.5, ALU.min, ALU.mult))
                if n >= 2:
                    dve.wait_ge(sem("f_act"), n - 1)
                dve.tensor_tensor(f_leaky[n % 2], h, f_neg[n % 2], ALU.add).then_inc(sem("f_leaky"), 1)
                for m in ([n - 3] if n % HB == 3 and n > 3 else []) + ([n] if n == 4 * HB - 1 else []):
                    done = m // HB if m != n else 4
                    c, e = (done - 1) // 2, (done - 1) % 2
                    dve.wait_ge(sem("f_pr"), HB * done)
                    for t in range(4):
                        tt = 4 * c + t
                        ins = dve.scalar_tensor_tensor(out=x[:, tt, :], in0=tiles2(2 * e + t // 2)[:, t % 2, :],
                                                       scalar=w_e[e][:, tt:tt + 1], in1=x[:, tt, :],
                                                       op0=ALU.mult, op1=ALU.add)
                        if t == 3:
                            ins.then_inc(sem("f_x"), 1)
                            dve.wait_ge(sem("f_x"), done)
            after(dve.memset(small[:, 72:80], 0.0))
            dve.tensor_copy(small[:, 72:80], small[:, 80:88]).then_inc(sem("x_done"), 1)
            norm_rows(3)
            dve.wait_ge(sem("ld_a"), 80)
            for j in range(4):
                dve.wait_ge(sem("a_vproj"), j + 1)
                dve.tensor_tensor(a_v[:, 2 * j:2 * j + 2, :], tiles2(j),
                                  a_bv.unsqueeze(1).to_broadcast([128, 2, D]), ALU.add).then_inc(sem("a_v"), 1)
            for t in range(NT):
                ins = dve.tensor_tensor(x[:, t, :], x[:, t, :], a_bo, ALU.add)
            after(ins)
            tops = [small[:, 56:64], small[:, 64:72]]
            dens2 = [small[:, 72:80], small[:, 80:88]]

            def a_divide(h):
                dve.wait_ge(sem("a_exp"), h + 1)
                e, dens = sm_e[h % 2], dens2[h % 2]
                after(dve.tensor_reduce(dens, e, AX.X, ALU.add))
                after(dve.reciprocal(dens, dens))
                dve.tensor_tensor(e, e, spread(dens), ALU.mult).then_inc(sem("a_p"), 1)

            for h in range(NH):
                s = ps[:, 4 + 2 * (h % 2), :].rearrange("p (a b) -> p a b", b=S)
                t = sm_t[h % 2]
                dve.wait_ge(sem("a_s"), h + 1)
                dve.scalar_tensor_tensor(out=t, in0=s, scalar=float(HDS) ** -0.5,
                                         in1=a_bias[:, h, :].unsqueeze(1).to_broadcast([128, NT, S]),
                                         op0=ALU.mult, op1=ALU.add).then_inc(sem("a_t"), 1)
                dve.wait_ge(sem("a_t"), h + 1)
                after(dve.tensor_reduce(tops[h % 2], t, AX.X, ALU.max))
                if h >= 2:
                    dve.wait_ge(sem("a_tr"), h - 1)
                dve.tensor_tensor(t, t, spread(tops[h % 2]), ALU.subtract).then_inc(sem("a_shift"), 1)
                if h >= 1:
                    a_divide(h - 1)
            a_divide(NH - 1)
            for g in range(4):
                r, j0 = g // 2, 2 * (g % 2)
                dve.wait_ge(sem("a_ctx"), NH)
                dve.tensor_copy(a_o.rearrange("p (j r) n -> p r j n", r=2)[:, r, j0:j0 + 2, :], tiles2(g))\
                    .then_inc(sem("a_o"), 1)
            add_tiles((sem("a_out"), [2, 4, 6, 8]))
            dve.wait_ge(sem("x_done"), 4)
            norm_rows(4)
            dve.wait_ge(sem("ld_t"), 48)
            for i in range(3):
                dve.tensor_reduce(small[:, 8 + i:9 + i], t_w[i], AX.X, ALU.add, apply_absolute_value=True)\
                    .then_inc(sem("t_abs"), 1)
            ws, iws = small[:, 16:19], small[:, 19:22]
            dve.wait_ge(sem("t_sum"), 1)
            after(dve.tensor_scalar(ws, ps[:, 4, 0:3], 1.0 / (HID * D), EPS, ALU.mult, ALU.add))
            dve.reciprocal(iws, ws).then_inc(sem("t_ws"), 1)
            dve.wait_ge(sem("ld_x1m"), 32)
            after(dve.tensor_copy(mask_f, mask_u8))
            after(dve.tensor_scalar(mask_add, mask_f, 1.0, -NEG, ALU.subtract, ALU.mult))
            cross(1)
            dve.wait_ge(sem("x_done"), 5)
            norm_rows(5)
            dve.wait_ge(sem("ln_xn"), 48)
            xs, xrs = small[:, 24:32], small[:, 32:40]
            g_sc, u_sc = small[:, 56:64], small[:, 64:72]
            after(dve.tensor_reduce(xs, xn[:, :, :], AX.X, ALU.max, apply_absolute_value=True))
            after(dve.tensor_scalar(xs, xs, 1.0 / 127.0, EPS, ALU.mult, ALU.add))
            after(dve.reciprocal(xrs, xs))
            for t in range(NT):
                ins = dve.tensor_scalar(t_xr[:, t, :], xn[:, t, :], xrs[:, t:t + 1], 127.0, ALU.mult, ALU.min)
            after(ins)
            after(dve.tensor_scalar(t_xr, t_xr, -128.0, MAGIC, ALU.max, ALU.add))
            dve.tensor_scalar(t_xq, t_xr, MAGIC, None, ALU.subtract).then_inc(sem("t_xq"), 1)
            after(dve.tensor_scalar(g_sc, xs, ws[:, 0:1], None, ALU.mult))
            dve.tensor_scalar(u_sc, xs, ws[:, 1:2], None, ALU.mult).then_inc(sem("t_sc"), 1)
            dve.wait_ge(sem("t_sc"), 1)
            hs, hr, dn = small[:, 72:80], small[:, 80:88], small[:, 88:96]
            for t in range(NT + 1):
                if t < NT:
                    h = t_h[t % 2]
                    dve.wait_ge(sem("t_gate"), t + 1)
                    dve.scalar_tensor_tensor(out=h, in0=pair(2), scalar=u_sc[:, t:t + 1], in1=t_gate[t % 2],
                                             op0=ALU.mult, op1=ALU.mult).then_inc(sem("t_prod"), 1)
                    dve.wait_ge(sem("t_prod"), t + 1)
                    c = slice(t, t + 1)
                    after(dve.tensor_reduce(hs[:, c], h, AX.X, ALU.max, apply_absolute_value=True))
                    after(dve.tensor_scalar(hs[:, c], hs[:, c], 1.0 / 127.0, EPS, ALU.mult, ALU.add))
                    after(dve.reciprocal(hr[:, c], hs[:, c]))
                    after(dve.tensor_scalar(t_r, h, hr[:, c], 127.0, ALU.mult, ALU.min))
                    after(dve.tensor_scalar(t_r, t_r, -128.0, MAGIC, ALU.max, ALU.add))
                    if t >= 2:
                        dve.wait_ge(sem("t_htr"), t - 1)
                    dve.tensor_scalar(t_hq[t % 2], t_r, MAGIC, None, ALU.subtract).then_inc(sem("t_hq"), 1)
                    after(dve.tensor_tensor(dn[:, c], hs[:, c], ws[:, 2:3], ALU.mult))
                if t >= 1:
                    dve.wait_ge(sem("t_dn"), t)
                    dve.scalar_tensor_tensor(out=x[:, t - 1, :], in0=ps[:, 5 + (t - 1) % 2, 0:D],
                                             scalar=dn[:, t - 1:t], in1=x[:, t - 1, :],
                                             op0=ALU.mult, op1=ALU.add).then_inc(sem("y_done"), 1)


def layouts(i):
    import numpy as np

    def kparts(a):
        return a.reshape(-1, 128, a.shape[1]).transpose(1, 0, 2)

    def heads(a, n):
        return a.reshape(n, 128, a.shape[1]).transpose(1, 0, 2)

    w = i["L0_attn_W_in"]
    cut = np.cumsum([DI, DXB, DXB, DI])
    z, xb, bm, cm, dt = np.split(w, cut, axis=0)
    cm = cm.reshape(NK, 8, 4, 4, D).transpose(0, 2, 1, 3, 4).reshape(DI, D)
    xb = np.broadcast_to(xb.reshape(NK, 1, 16, D), (NK, 8, 16, D)).reshape(DI, D)
    win = np.concatenate([z, xb, bm, cm, dt], axis=0).T

    def chan(a):
        return a.reshape(NK, 128, -1).transpose(1, 0, 2)

    zero = np.zeros((DI, 1), np.float32)
    mpar = np.concatenate([i["L0_attn_conv_w"].reshape(DI, DCONV), i["L0_attn_conv_b"][:, None],
                           i["L0_attn_D_param"][:, None], i["L0_attn_b_dt"][:, None], zero], axis=1)
    ctx = i["ctx_1024"]
    ctxn = ctx.reshape(4, 2, 2, S, CD).transpose(1, 3, 0, 2, 4).reshape(128, NT, CD)
    row = np.arange(96)[:, None] % 32
    sel_b = np.repeat((row == np.arange(32)[None, :])[:, :, None], 128, axis=2)
    sel_c = row[:, :, None] == 4 * (np.arange(128)[None, None, :] // 16) + np.arange(4)[None, :, None]
    pos = np.arange(1 - S, 1)
    slope = 0.5 ** (np.arange(1, NH + 1) * (8.0 / NH))
    causal = np.arange(S)[None, None, :] <= (np.arange(128) % S)[:, None, None]
    a_bias = np.where(causal, (slope[:, None] * pos[None, :])[None], NEG)
    qkv, bqkv = i["L1_attn_Wqkv"], i["L1_attn_b_qkv"]
    bf16 = np.dtype("bfloat16")
    eye = np.eye(128)
    r = {
        "x": i["x"].reshape(NT, 128, D).transpose(1, 0, 2),
        "ctxT": ctx.reshape(TOK, CD).T, "ctxn": ctxn,
        "mask": np.asarray(i["mask_BxS2_bf1"]).view(np.uint8),
        "ident": eye.astype(np.float32), "identb": eye.astype(bf16), "ones": np.ones((128, 128), np.float32),
        "sel_b": sel_b.astype(bf16), "sel_c": sel_c.astype(bf16),
        "head_mask": (np.arange(128)[:, None] // HDS == np.arange(8)[None, :]).astype(np.float32),
        "a_bias": a_bias.astype(np.float32),
        "m_win": kparts(win), "m_wdt": i["L0_attn_W_dt"].T, "m_wout": kparts(i["L0_attn_W_out"].T),
        "a_log": chan(i["L0_attn_A_log"]), "mpar": chan(mpar),
        "g": np.stack([i["L0_xattn_gq"], i["L0_xattn_gk"]], axis=1),
        "x0_wq": kparts(i["L0_xattn_Wq"]), "x0_wk": i["L0_xattn_Wk"],
        "x0_wvT": i["L0_xattn_Wv"].reshape(CD, NH, HD).transpose(2, 1, 0), "x0_wo": heads(i["L0_xattn_Wo"], NH),
        "f_router": kparts(i["L0_ffn_w_router"].T),
        "f_fc": kparts(i["L0_ffn_w_fc"].reshape(2 * HID, D).T),
        "f_proj": kparts(i["L0_ffn_w_proj"].transpose(0, 2, 1).reshape(2 * HID, D)),
        "a_wqkv": kparts(qkv.T), "a_wout": kparts(i["L1_attn_Wout"].T),
        "a_bqk": bqkv[:2 * D].reshape(4, 128).T, "a_bv": bqkv[2 * D:], "a_bo": i["L1_attn_b_out"],
        "x1_wqT": i["L1_xattn_Wq"].reshape(D, NH, HD).transpose(2, 1, 0),
        "x1_wkT": i["L1_xattn_Wk"].reshape(CD, NKV, HD).transpose(2, 1, 0),
        "x1_wvT": i["L1_xattn_Wv"].reshape(CD, NKV, HD).transpose(2, 1, 0), "x1_wo": heads(i["L1_xattn_Wo"], NH),
        "t_gate": kparts(i["L1_ffn_w_gate"].T).reshape(128, -1), "t_up": kparts(i["L1_ffn_w_up"].T).reshape(128, -1),
        "t_down": kparts(i["L1_ffn_w_down"].T).reshape(128, -1),
    }
    return {k: np.ascontiguousarray(v) for k, v in r.items()}


def kernel(**inputs):
    import numpy as np
    import concourse.bacc as bacc
    from concourse.bass_utils import run_bass_kernel_spmd

    nc = bacc.Bacc("TRN2", target_bir_lowering=False, num_devices=1)
    arrays, io = {}, {}
    for name, a in layouts({k: np.asarray(v) for k, v in inputs.items()}).items():
        arrays[f"in_{name}"] = a
        io[name] = nc.dram_tensor(f"in_{name}", a.shape, mybir.dt.from_np(a.dtype), kind="ExternalInput").ap()
    out = nc.dram_tensor("out_x", (128, NT, D), F32, kind="ExternalOutput").ap()
    program(nc, io, out)
    got = run_bass_kernel_spmd(nc, [arrays], core_ids=[0]).results[0]["out_x"]
    return np.ascontiguousarray(np.asarray(got).transpose(1, 0, 2)).reshape(B, S, D)
```

```python
from contextlib import ExitStack

import concourse.bass as bass
from concourse import mybir

F32 = mybir.dt.float32
BF16 = mybir.dt.bfloat16
U8 = mybir.dt.uint8
ALU = mybir.AluOpType
ACT = mybir.ActivationFunctionType
AX = mybir.AxisListType

B, S, D = 16, 64, 256
TOK = B * S
NT = TOK // 128
KH = D // 128
HALF = TOK // 2
EPS = 1e-5
DI, DXB, DST, DCONV, DTR = 512, 64, 16, 4, 128
NK = DI // 128
CD, HD, NH = 128, 128, 16
NKV = 8
HID = 1024
HB = HID // 128
HDS = D // NH
M_X, M_B, M_C, M_DT = DI, 2 * DI, 2 * DI + DXB, 3 * DI + DXB
M_COLS = M_DT + DTR
MAGIC = 1.5 * 2.0 ** 23
NEG = -1e30
QSCALE = float(HD) ** -0.5
LOG1P_SPLIT = 2.0 ** -8


class Counted:

    def __init__(self, sem):
        self.sem, self.n = sem, 0

    def on(self, ins):
        ins.then_inc(self.sem, 1)
        self.n += 1
        return ins


def work_turns(order):
    seen, turns = {"act": 0, "dve": 0}, {}
    for w, (job, by) in enumerate(order):
        seen[by] += 1
        turns[job] = (w, by, seen[by])
    return turns


def program(nc, io, out):
    ctx = ExitStack()
    with ctx:
        def sb(name, shape, dt=F32):
            return ctx.enter_context(nc.sbuf_tensor(name, shape, dt))

        sems = {}

        def sem(name):
            if name not in sems:
                sems[name] = ctx.enter_context(nc.semaphore(name))
            return sems[name]

        ident = sb("ident", [128, 128])
        identb = sb("identb", [128, 128], BF16)
        ones = sb("ones", [128, 128])
        sel_b = sb("sel_b", [96, 32, 128], BF16)
        sel_c = sb("sel_c", [96, 4, 128], BF16)
        x = sb("x", [128, NT, D])
        xn = sb("xn", [128, NT, D])
        xnT = sb("xnT", [128, KH, TOK])
        ctxT = sb("ctxT", [128, TOK])
        ctxn = sb("ctxn", [128, NT, CD])
        stats = sb("stats", [128, NT, 6])
        mv = sb("mv", [128, NT, 2])
        rstd = sb("rstd", [128, NT])
        small = sb("small", [128, 160])
        head_mask = sb("head_mask", [128, 8])
        a_log = sb("a_log", [128, NK, DST])
        mpar = sb("mpar", [128, NK, 8])
        qkb = sb("qkb", [128, 4])
        ps = ctx.enter_context(nc.psum_tensor("ps", [128, 8, 512], F32))
        region = {"A": sb("region_a", [128, 48 * 256]), "B": sb("region_b", [128, 48 * 256]),
                  "C": sb("region_c", [128, 64 * 256])}

        def view(name, kb, shape, dt=F32, rows=128):
            size = 4 if dt == F32 else 2 if dt == BF16 else 1
            n = 1
            for d in shape:
                n *= d
            a = int(kb * 256)
            words = n * size // 4
            v = region[name][0:rows, a:a + words]
            if dt != F32:
                v = v.bitcast(dt)
            if len(shape) == 2:
                v = v.rearrange("p (a b) -> p a b", b=shape[1])
            if len(shape) == 3:
                v = v.rearrange("p (a b c) -> p a b c", b=shape[1], c=shape[2])
            return v

        eps_col = small[:, 0:1]
        one_col = small[:, 1:2]
        gq_col, gk_col, g_col = small[:, 3:4], small[:, 4:5], small[:, 5:6]

        m_win = view("B", 0, [KH, M_COLS])
        m_wdt = view("B", 14, [DI])
        m_wout = view("B", 16, [NK, D])
        m_sb = view("B", 20, [2, TOK], BF16, 96)
        m_sc = [view("B", 24 + 8 * i, [4, TOK], BF16, 96) for i in range(2)]
        m_part = [view("B", 40 + 2 * i, [TOK], BF16) for i in range(3)]
        m_rest, m_dtl, m_e, m_ln, m_dtx, m_acc = [view("A", 4 * i, [TOK]) for i in range(6)]
        m_da = [view("C", 4 * i, [B, S]) for i in range(2)]
        m_dbu = [view("C", 8 + 4 * i, [TOK]) for i in range(2)]
        m_h = [view("C", 16 + 4 * i, [TOK]) for i in range(2)]
        m_hc = [view("C", 24 + 4 * i, [TOK]) for i in range(2)]
        m_u = view("C", 32, [NK, TOK])
        m_delta = [view("C", 48 + 4 * i, [B, S]) for i in range(2)]
        m_du = view("C", 56, [TOK])
        m_zs = view("C", 60, [TOK])
        wq = view("A", 0, [KH, NH * HD])
        wk = view("A", 16, [NH * HD])
        wvT = view("A", 24, [NH, CD])
        wo = view("A", 32, [NH, D])
        wqT1 = view("A", 0, [NH, D])
        wkT1 = view("A", 16, [NKV, CD])
        wvT1 = view("A", 20, [NKV, CD])
        wo1 = view("A", 24, [NH, D])
        wvo = view("C", 0, [NH, D])
        k_gain = view("C", 16, [TOK])
        k_sq = view("C", 20, [TOK])
        k_rn = view("C", 24, [TOK])
        k_T = [view("C", 28 + 4 * i, [TOK]) for i in range(2)]
        q_sq = view("C", 36, [TOK])
        wqk = view("C", 16, [NH, KH, CD])
        mask_add = view("C", 32, [B, S])
        mask_f = view("C", 36, [B, S])
        q_T = view("C", 40, [2 * TOK])
        sm_t = view("C", 48, [B, S])
        sm_e = view("C", 52, [B, S])
        mask_u8 = view("C", 52, [B, S], U8)
        o_T = view("C", 56, [2, TOK])
        p_T = view("B", 44, [2, 512])
        f_fc = view("B", 0, [KH, 2 * HID])
        f_proj = view("B", 16, [2 * HB, D])
        f_neg = [view("C", 2 * i, [HALF]) for i in range(2)]
        f_leaky = [view("C", 4 + 2 * i, [HALF]) for i in range(2)]
        f_act = [view("C", 8 + 2 * i, [HALF]) for i in range(4)]
        f_router = view("B", 40, [KH, 2])
        a_wqkv = view("B", 32, [KH, 3 * D])
        a_wout = view("B", 38, [KH, D])
        a_bias = view("A", 40, [NH, S])
        a_bv = view("A", 44, [D])
        a_bo = view("A", 45, [D])
        a_q = view("C", 0, [KH, TOK])
        a_k = view("C", 8, [KH, TOK])
        a_v = view("C", 16, [NT, D])
        a_qm = [view("C", 24 + 4 * i, [TOK]) for i in range(2)]
        a_o = view("C", 0, [NT, D])
        a_oT = view("C", 8, [KH, TOK])
        a_t = [view("C", 40 + 4 * i, [NT, S]) for i in range(2)]
        a_e = [view("C", 42 + 4 * i, [NT, S]) for i in range(2)]
        a_pT = view("C", 48, [4, 128])
        t_w = [view("B", 8 * i, [2048]) for i in range(3)]
        t_wq = [view("B", kb, [2048], BF16) for kb in (24, 28, 40)]
        t_gate_q = t_wq[0].rearrange("p (k n) -> p k n", k=KH)
        t_up_q = t_wq[1].rearrange("p (k n) -> p k n", k=KH)
        t_down_q = t_wq[2].rearrange("p (k n) -> p k n", k=HB)
        t_xr = view("C", 0, [NT, D])
        t_xq = view("C", 8, [NT, D], BF16)
        t_xqT = view("C", 12, [KH, TOK], BF16)
        t_gate = [view("C", 16 + 4 * i, [HID]) for i in range(2)]
        t_h = [view("C", 24 + 4 * i, [HID]) for i in range(2)]
        t_hq = [view("C", 32 + 2 * i, [HID], BF16) for i in range(2)]
        t_hqT = view("C", 36, [HB, 128], BF16)
        t_r = view("C", 40, [HID])

        def tiles2(a):
            return ps[:, a, :].rearrange("p (t n) -> p t n", t=2)

        def pair(a):
            return ps[:, a:a + 2, :].rearrange("p a n -> p (a n)")

        def spread(col8):
            return col8.unsqueeze(2).to_broadcast([128, NT, S])

        def proj_no(what, k):
            if what == "low rank":
                return 1
            if what == "B":
                return 2
            if k == 0 and what != "z":
                return {"u": 3, "C": 4, "dt": 5}[what]
            if what == "z":
                return 9 + 4 * k if k < NK - 1 else 6 + 4 * k
            return 5 + 4 * (k - 1) + {"dt": 1, "u": 2, "C": 3}[what]

        PROJ_PAIR = {"u": 4, "C": 6, "dt": 0}
        def proj_pair(what, k):
            return PROJ_PAIR[what] if k == 0 and what != "z" else 6

        def head_order(layer):
            order = [(("wvo", i, 0), "dve") for i in range(NH // 2)]
            if layer == 1:
                order += [(("wqk", i, 0), "act") for i in range(NH // 2)]
            for i in range(NH // 2 + 1):
                if i < NH // 2:
                    for a in range(2):
                        order += [(("q", 2 * i + a, c), "act") for c in range(2)]
                        if layer == 0:
                            order += [(("k", 2 * i + a, c), "act") for c in range(2)]
                            order += [(("ss", 2 * i + a, c), "act") for c in range(2)]
                            order += [(("qn", 2 * i + a, 0), "act")]
                if i >= 1:
                    order += [(("pT", i - 1, a), "dve") for a in range(2)]
                    order += [(("o", i - 1, n), "act") for n in range(4)]
            return order

        TURNS = [work_turns(head_order(0)), work_turns(head_order(1))]
        
        block = ctx.enter_context(nc.Block())

        @block.sync
        def _(sp):
            def load(dst, src, name):
                sp.dma_start(dst, src).then_inc(sem(name), 16)

            for g in range(4):
                load(x[:, 2 * g:2 * g + 2, :], io["x"][:, 2 * g:2 * g + 2, :], f"ld_rows{g}")
            for k in range(KH):
                load(m_win[:, k, :], io["m_win"][:, k, :], "ld_m")
            for dst, name in ((ident, "ident"), (ones, "ones"), (identb, "identb"), (sel_c, "sel_c"), (sel_b, "sel_b"),
                              (a_log, "a_log"), (mpar, "mpar"), (head_mask, "head_mask")):
                load(dst[:], io[name], "ld_const")
            load(small[:, 3:5], io["g"], "ld_const")
            load(qkb[:, :], io["a_bqk"], "ld_const")
            load(m_wdt, io["m_wdt"], "ld_m")
            load(m_wout, io["m_wout"], "ld_m")
            load(wvT, io["x0_wvT"], "ld_x0")
            load(wo, io["x0_wo"], "ld_x0")
            load(ctxT[:, :], io["ctxT"], "ld_x0")
            load(ctxn[:, :, :], io["ctxn"], "ld_x0")
            for k in range(-1, NK):
                sp.wait_ge(sem("m_parts"), k + 2)
                if k < 0:
                    for part in range(3):
                        for a in range(2):
                            load(m_sb[32 * part:32 * part + 32, a, :], m_part[part][32 * a:32 * a + 32, :], "ld_sb")
                    sp.wait_ge(sem("ld_sb"), 96)
                else:
                    if k >= 2:
                        sp.wait_ge(sem("m_hc"), DST * (k - 1))
                    for part in range(3):
                        for a in range(4):
                            load(m_sc[k % 2][32 * part:32 * part + 32, a, :], m_part[part][32 * a:32 * a + 32, :], "ld_sc")
            sp.wait_ge(sem("m_delta"), NK)
            sp.wait_ge(sem("m_u"), NK)
            load(wq, io["x0_wq"], "ld_x0")
            load(wk, io["x0_wk"], "ld_x0")
            sp.wait_ge(sem("ln_xn"), 2 * NT)
            for name, dst in (("f_router", f_router), ("f_fc", f_fc), ("f_proj", f_proj)):
                load(dst, io[name], "ld_f")
            load(a_wqkv, io["a_wqkv"], "ld_a")
            load(a_wout, io["a_wout"], "ld_a")
            sp.wait_ge(sem("ln_xn"), 3 * NT)
            load(a_bias, io["a_bias"], "ld_a")
            load(a_bv, io["a_bv"].partition_broadcast(128), "ld_a")
            load(a_bo, io["a_bo"].partition_broadcast(128), "ld_a")
            for name, dst in (("x1_wvT", wvT1), ("x1_wo", wo1), ("x1_wqT", wqT1), ("x1_wkT", wkT1)):
                load(dst, io[name], "ld_x1")
            sp.wait_ge(sem("ln_xn"), 4 * NT)
            for i, name in enumerate(("t_gate", "t_up", "t_down")):
                load(t_w[i], io[name], "ld_t")
            sp.wait_ge(sem("ln_xn"), 5 * NT)
            load(mask_u8, io["mask"].partition_broadcast(128), "ld_x1m")
            for t in range(NT):
                sp.wait_ge(sem("y_done"), t + 1)
                sp.dma_start(out[:, t, :], x[:, t, :]).then_inc(sem("st_out"), 16)
            sp.wait_ge(sem("st_out"), 16 * NT)

        @block.gpsimd
        def _(pool):
            step = Counted(sem("pool_step"))
            for h in range(NH):
                pool.wait_ge(sem("a_qk"), 8)
                if h >= 2:
                    pool.wait_ge(sem("a_s"), h - 1)
                pool.tensor_scalar(a_qm[h % 2], a_q[:, h // 8, :], head_mask[:, h % 8:h % 8 + 1], None,
                                   ALU.mult).then_inc(sem("a_qm"), 1)
            pool.wait_ge(sem("t_ws"), 1)
            for i in range(3):
                step.on(pool.tensor_scalar(t_w[i], t_w[i], small[:, 19 + i:20 + i], 1.0, ALU.mult, ALU.min))
                pool.wait_ge(step.sem, step.n)
                step.on(pool.tensor_scalar(t_w[i], t_w[i], -1.0, MAGIC, ALU.max, ALU.add))
                pool.wait_ge(step.sem, step.n)
                pool.tensor_scalar(t_wq[i], t_w[i], MAGIC, None, ALU.subtract).then_inc(sem("t_wq"), 1)

        @block.scalar
        def _(act):
            step = Counted(sem("act_step"))

            def after(ins):
                step.on(ins)
                act.wait_ge(step.sem, step.n)

            def norm_rows(ln, transposed=True):
                for g in range(4):
                    act.wait_ge(sem("ln_var"), 4 * ln + g + 1)
                    r = rstd[:, 2 * g:2 * g + 2]
                    after(act.activation(r, mv[:, 2 * g:2 * g + 2, 1], ACT.Ln, bias=eps_col))
                    act.activation(r, r, ACT.Exp, scale=-0.5).then_inc(sem("ln_rstd"), 1)
                if transposed:
                    for g in range(4):
                        act.wait_ge(sem("ln_tr"), 4 * ln + g + 1)
                        act.activation(xnT[:, :, 256 * g:256 * g + 256], tiles2(g), ACT.Copy)\
                            .then_inc(sem("ln_T"), 1)

            def exp_tables():
                act.preload_act_table_set("natural_log_exp_and_others")

            exp_tables()
            act.wait_ge(sem("ready"), 1)
            norm_rows(0)
            act.wait_ge(sem("ld_const"), 160)
            act.activation(a_log[:, :, :], a_log[:, :, :], ACT.Exp).then_inc(sem("m_aexp"), 1)
            def done(what, k):
                act.wait_ge(sem("m_proj"), proj_no(what, k))
                return pair(proj_pair(what, k))

            def part0(src, rows, count):
                if count == 1:
                    act.wait_ge(sem("ld_sb"), 96)
                if count >= 2:
                    act.wait_ge(sem("ld_sc"), 192 * (count - 1))
                act.activation(m_part[0][0:rows], src[0:rows], ACT.Copy).then_inc(sem("m_p0"), 1)

            def part1(rows, count):
                act.wait_ge(sem("m_r1"), count + 1)
                act.activation(m_part[1][0:rows], m_rest[0:rows], ACT.Copy).then_inc(sem("m_p1"), 1)

            def step_in(k):
                src = done("dt", k)
                if k == 0:
                    act.wait_ge(sem("m_b2"), 1)
                else:
                    act.wait_ge(sem("m_delta"), k)
                act.activation(m_dtx, src, ACT.Identity, bias=mpar[:, k, 7:8])
                act.activation(m_e, src, ACT.Abs, bias=mpar[:, k, 7:8]).then_inc(sem("m_ax"), 1)

            def step_log(k):
                act.wait_ge(sem("m_ax"), k + 1)
                after(act.activation(m_e, m_e, ACT.Exp, scale=-1.0))
                act.activation(m_ln, m_e, ACT.Ln, bias=one_col).then_inc(sem("m_ln"), 1)

            def channels(k):
                act.wait_ge(sem("m_conv"), k + 1)
                act.activation(m_u[:, k, :], m_acc, ACT.Silu, bias=mpar[:, k, 4:5]).then_inc(sem("m_u"), 1)

            act.wait_ge(sem("m_proj"), 1)
            act.activation(m_dtl, pair(0), ACT.Copy).then_inc(sem("m_dtl"), 1)
            act.wait_ge(sem("m_proj"), 2)
            part0(pair(2), 64, 0)
            part1(64, 0)
            part0(done("C", 0), 128, 1)
            part1(128, 1)
            step_in(0)
            step_log(0)
            channels(0)
            exp_tables()
            for u in range(NK * DST):
                k, n = u // DST, u % DST
                if n == 0:
                    act.wait_ge(sem("m_delta"), k + 1)
                if u >= 2:
                    act.wait_ge(sem("m_scan"), u - 1)
                act.activation(m_da[n % 2][:, :, 1:S], m_delta[k % 2][:, :, 1:S], ACT.Exp,
                               scale=a_log[:, k, n:n + 1]).then_inc(sem("m_da"), 1)
                if k < NK - 1:
                    if n == 2:
                        step_in(k + 1)
                    if n == 3:
                        step_log(k + 1)
                    if n == 10:
                        part0(done("C", k + 1), 128, k + 2)
                    if n == 12:
                        part1(128, k + 2)
                    if n == DST - 1:
                        channels(k + 1)
                if n == DST - 1:
                    z = done("z", k)
                    act.wait_ge(sem("m_yg"), k)
                    if k < NK - 1:
                        act.wait_ge(sem("m_delta"), k + 2)
                    act.activation(m_zs, z, ACT.Silu).then_inc(sem("m_zs"), 1)
                    exp_tables()

            def cross(layer):
                turns, tag = TURNS[layer], f"x{layer}"
                filled, freed = sem(tag + "_filled"), sem(tag + "_free_act")

                def bank(job):
                    w = turns[job][0]
                    act.wait_ge(filled, w + 1)
                    return ps[:, 6 + w % 2, :]

                if layer == 1:
                    for i in range(NH // 2):
                        b = bank(("wqk", i, 0))
                        act.activation(wqk[:, 2 * i:2 * i + 2].rearrange("p a b c -> p (a b c)"), b,
                                       ACT.Copy).then_inc(freed, 1)

                def exps(i):
                    act.wait_ge(sem(tag + "_shift"), i + 1)
                    act.activation(sm_e, sm_t, ACT.Exp).then_inc(sem(tag + "_exp"), 1)

                def queries(h):
                    for c in range(2):
                        b = bank(("q", h, c))
                        if layer == 0:
                            act.activation(q_sq[:, c * HALF:c * HALF + HALF], b, ACT.Square)
                            a = h % 2 * TOK + c * HALF
                            act.activation(q_T[:, a:a + HALF], b, ACT.Copy).then_inc(freed, 1)
                        else:
                            dst = q_T.rearrange("p (b a q) -> p b a q", a=2, q=S)[:, 8 * c:8 * c + 8, h % 2, :]
                            act.activation(dst, b.rearrange("p (b q) -> p b q", q=S), ACT.Copy).then_inc(freed, 1)

                def keys(h):
                    if h >= 1:
                        act.wait_ge(sem("x0_kT"), 2 * h)
                    for c in range(2):
                        cs = slice(c * HALF, c * HALF + HALF)
                        b = bank(("k", h, c))
                        act.activation(k_sq[:, cs], b, ACT.Square)
                        act.activation(k_gain[:, cs], b, ACT.Copy, scale=g_col).then_inc(freed, 1)

                def norms(h):
                    for c in range(2):
                        cs = slice(c * HALF, c * HALF + HALF)
                        b = bank(("ss", h, c))
                        act.activation(k_rn[:, cs], b, ACT.Ln, scale=1.0 / HD, bias=eps_col).then_inc(freed, 1)
                        act.wait_ge(freed, turns[("ss", h, c)][2])
                        act.activation(k_rn[:, cs], k_rn[:, cs], ACT.Exp, scale=-0.5).then_inc(sem("x0_rk"), 1)
                    b = bank(("qn", h, 0))
                    lnq = small[:, 96 + 8 * (h % 2):104 + 8 * (h % 2)]
                    act.activation(lnq, b[:, 0:8], ACT.Ln, scale=1.0 / HD, bias=eps_col).then_inc(freed, 1)
                    act.wait_ge(freed, turns[("qn", h, 0)][2])
                    if h >= 2:
                        act.wait_ge(sem("x0_t"), h // 2)
                    act.activation(small[:, 112 + 8 * (h % 2):120 + 8 * (h % 2)], lnq, ACT.Exp, scale=-0.5)\
                        .then_inc(sem("x0_rq"), 1)

                for i in range(NH // 2 + 1):
                    for a in range(2):
                        h = 2 * i + a
                        if h < NH:
                            queries(h)
                        if i >= 1 and a == 0:
                            exps(i - 1)
                        if h < NH and layer == 0:
                            keys(h)
                            norms(h)
                    if i >= 1:
                        for n in range(4):
                            b = bank(("o", i - 1, n))
                            r, jh = n % 2, n // 2
                            dst = o_T.rearrange("p a (j r n) -> p r a j n", r=2, n=128)[:, r, :, 2 * jh:2 * jh + 2]
                            act.activation(dst, b.rearrange("p (a j n) -> p a j n", a=2, j=2), ACT.Copy)\
                                .then_inc(freed, 1)

            norm_rows(1)
            act.wait_ge(sem("x0_g"), 1)
            cross(0)
            norm_rows(2)
            act.wait_ge(sem("f_ld"), 1)
            act.activation(small[:, 24:32], small[:, 16:24], ACT.Exp, scale=-1.0).then_inc(sem("f_e"), 1)
            for n in range(4 * HB):
                act.wait_ge(sem("f_leaky"), n + 1)
                if n >= 4:
                    act.wait_ge(sem("f_pr"), n - 3)
                act.activation(f_act[n % 4], f_leaky[n % 2], ACT.Square).then_inc(sem("f_act"), 1)
            norm_rows(3)
            for n in range(8):
                act.wait_ge(sem("a_proj"), n + 1)
                dst = (a_q if n < 4 else a_k)[:, n // 2 % 2, HALF * (n % 2):HALF * (n % 2) + HALF]
                act.activation(dst, ps[:, 4 + n % 4, :], ACT.Identity, bias=qkb[:, n // 2:n // 2 + 1])\
                    .then_inc(sem("a_qk"), 1)
            for i in range(NH + 2):
                if i < NH:
                    act.wait_ge(sem("a_shift"), i + 1)
                    act.activation(a_e[i % 2], a_t[i % 2], ACT.Exp).then_inc(sem("a_exp"), 1)
                if i >= 2:
                    act.wait_ge(sem("a_tr"), i - 1)
                    act.activation(a_pT, ps[:, 5, :].rearrange("p (a b) -> p a b", a=4), ACT.Copy)\
                        .then_inc(sem("a_pT"), 1)
            for g in range(4):
                act.wait_ge(sem("a_otr"), g + 1)
                act.activation(a_oT[:, :, 256 * g:256 * g + 256], tiles2(4 + g), ACT.Copy)\
                    .then_inc(sem("a_oT"), 1)
            norm_rows(4)
            cross(1)
            norm_rows(5, transposed=False)
            for g in range(2):
                act.wait_ge(sem("t_xtr"), g + 1)
                act.activation(t_xqT[:, :, HALF * g:HALF * g + HALF],
                               ps[:, 2 * g, :].bitcast(BF16).rearrange("p (k n) -> p k n", k=KH), ACT.Copy)\
                    .then_inc(sem("t_xT"), 1)
            for t in range(NT + 1):
                if t < NT:
                    act.wait_ge(sem("t_gu"), t + 1)
                    act.wait_ge(sem("t_sc"), 1)
                    if t >= 2:
                        act.wait_ge(sem("t_prod"), t - 1)
                    act.activation(t_gate[t % 2], pair(0), ACT.Silu, scale=small[:, 56 + t:57 + t])\
                        .then_inc(sem("t_gate"), 1)
                if t >= 1:
                    act.wait_ge(sem("t_htr"), t)
                    act.activation(t_hqT, ps[:, 4, :].bitcast(BF16).rearrange("p (k n) -> p k n", k=HB),
                                   ACT.Copy).then_inc(sem("t_hT"), 1)

        @block.tensor
        def _(pe):
            def norm_rows(ln):
                for g in range(4):
                    pe.wait_ge(sem("ln_xn"), 8 * ln + 2 * g + 2)
                    for k in range(KH):
                        for a in range(2):
                            last = pe.transpose(tiles2(g)[:, k, 128 * a:128 * a + 128],
                                                xn[:, 2 * g + a, 128 * k:128 * k + 128], ident[:, :])
                    last.then_inc(sem("ln_tr"), 1)
                pe.wait_ge(sem("ln_T"), 4 * ln + 4)

            pe.wait_ge(sem("ld_const"), 160)
            norm_rows(0)
            pe.wait_ge(sem("ld_m"), 64)

            def project(pair_at, lhs, rows=128, rhs=None, halves=KH, cs=(0, 1)):
                for c in cs:
                    for k in range(halves):
                        last = pe.matmul(ps[0:rows, pair_at + c, :], lhs(k),
                                         (rhs if rhs is not None else xnT[:, k, :])[:, c * HALF:c * HALF + HALF],
                                         start=(k == 0), stop=(k == halves - 1))
                if cs[-1] == 1:
                    last.then_inc(sem("m_proj"), 1)

            def steps(k):
                project(proj_pair("dt", k), lambda _: m_wdt[:, 128 * k:128 * k + 128], 128, m_dtl, 1)

            def columns(what, k, cs=(0, 1)):
                a = {"u": M_X, "C": M_C, "z": 0}[what] + 128 * k
                project(proj_pair(what, k), lambda kh: m_win[:, kh, a:a + 128], cs=cs)

            project(0, lambda k: m_win[:, k, M_DT:M_COLS])
            project(2, lambda k: m_win[:, k, M_B:M_C], 64)
            columns("u", 0)
            columns("C", 0)
            pe.wait_ge(sem("m_dtl"), 1)
            steps(0)

            def put_b(u):
                if u == 0:
                    pe.wait_ge(sem("m_ax"), 1)
                    pe.wait_ge(sem("ld_sb"), 96)
                else:
                    pe.wait_ge(sem("m_dbu"), u)
                for c in range(2):
                    last = pe.matmul(ps[:, c, :], sel_b[:, u % 32, :], m_sb[:, u // 32, c * HALF:c * HALF + HALF],
                                     start=True, stop=True)
                last.then_inc(sem("m_b"), 1)

            def put_c(u):
                k, n = u // DST, u % DST
                if u == 0:
                    pe.wait_ge(sem("m_r1"), 1)
                else:
                    pe.wait_ge(sem("m_hc"), u)
                if n == 0:
                    pe.wait_ge(sem("ld_sc"), 192 * (k + 1))
                for c in range(2):
                    last = pe.matmul(ps[:, 2 + c, :], sel_c[:, n % 4, :],
                                     m_sc[k % 2][:, n // 4, c * HALF:c * HALF + HALF], start=True, stop=True)
                last.then_inc(sem("m_c"), 1)

            def add_state(u):
                k, n = u // DST, u % DST
                pe.wait_ge(sem("m_hc"), u + 1)
                if u == 0:
                    pe.wait_ge(sem("m_conv"), 1)
                elif n == 0:
                    pe.wait_ge(sem("m_yd"), k)
                for c in range(2):
                    last = pe.matmul(ps[:, 4 + c, :], ident[:, :], m_hc[n % 2][:, c * HALF:c * HALF + HALF],
                                     start=(n == 0), stop=(n == DST - 1))
                last.then_inc(sem("m_y"), 1)

            put_b(0)
            for u in range(NK * DST):
                k, n = u // DST, u % DST
                put_c(u)
                if u >= 1:
                    add_state(u - 1)
                if u + 1 < NK * DST:
                    put_b(u + 1)
                if k < NK - 1:
                    if n == 1:
                        if k == 0:
                            pe.wait_ge(sem("m_r1"), 2)
                        else:
                            pe.wait_ge(sem("m_zs"), k)
                        steps(k + 1)
                    if n in (3, 4):
                        pe.wait_ge(sem("m_ax"), k + 2)
                        columns("u", k + 1, (n - 3,))
                    if n in (7, 9):
                        pe.wait_ge(sem("m_conv"), k + 2)
                        columns("C", k + 1, ((n - 7) // 2,))
                if n in (12, 14):
                    if k < NK - 1:
                        pe.wait_ge(sem("m_r1"), k + 3)
                    else:
                        pe.wait_ge(sem("m_zs"), k)
                    columns("z", k, ((n - 12) // 2,))
            add_state(NK * DST - 1)
            pe.wait_ge(sem("m_yg"), NK)
            for t in range(NT):
                for k in range(NK):
                    last = pe.matmul(tiles2(t // 2)[:, t % 2, :], m_u[:, k, 128 * t:128 * t + 128], m_wout[:, k, :],
                                     start=(k == 0), stop=(k == NK - 1))
                last.then_inc(sem("m_out"), 1)

            def cross(layer):
                turns, tag = TURNS[layer], f"x{layer}"
                by_turn = {w: (by, n) for w, by, n in turns.values()}
                pe.wait_ge(sem("ld_" + tag), 96 if layer == 0 else 64)

                def bank(job):
                    w = turns[job][0]
                    if w >= 2:
                        by, n = by_turn[w - 2]
                        pe.wait_ge(sem(f"{tag}_free_{by}"), n)
                    return ps[:, 6 + w % 2, :]

                filled = sem(tag + "_filled")
                wv_h, wo_h = (wvT, wo) if layer == 0 else (wvT1, wo1)
                for i in range(NH // 2):
                    b = bank(("wvo", i, 0))
                    for a in range(2):
                        h = 2 * i + a
                        last = pe.matmul(b[:, 256 * a:256 * a + 256], wv_h[:, h if layer == 0 else h // 2, :],
                                         wo_h[:, h, :], start=True, stop=True)
                    last.then_inc(filled, 1)
                if layer == 1:
                    for i in range(NH // 2):
                        b = bank(("wqk", i, 0))
                        for a in range(2):
                            for k in range(KH):
                                c = (2 * a + k) * 128
                                last = pe.matmul(b[:, c:c + 128], wqT1[:, 2 * i + a, 128 * k:128 * k + 128],
                                                 wkT1[:, i, :], start=True, stop=True)
                        last.then_inc(filled, 1)

                def queries(h):
                    for c in range(2):
                        b = bank(("q", h, c))
                        for k in range(KH):
                            w = wq[:, k, HD * h:HD * h + HD] if layer == 0 else wqk[:, h, k, :]
                            last = pe.matmul(b, w, xnT[:, k, c * HALF:c * HALF + HALF],
                                             start=(k == 0), stop=(k == KH - 1))
                        last.then_inc(filled, 1)

                def keys(h):
                    for c in range(2):
                        b = bank(("k", h, c))
                        pe.matmul(b, wk[:, HD * h:HD * h + HD], ctxT[:, c * HALF:c * HALF + HALF],
                                  start=True, stop=True).then_inc(filled, 1)

                def norms(h):
                    for c in range(2):
                        b = bank(("ss", h, c))
                        pe.wait_ge(sem("x0_free_act"), turns[("k", h, c)][2])
                        pe.matmul(b, ones[:, :], k_sq[:, c * HALF:c * HALF + HALF],
                                  start=True, stop=True).then_inc(filled, 1)
                    b = bank(("qn", h, 0))
                    for t in range(NT):
                        last = pe.matmul(b[:, t:t + 1], q_sq[:, 128 * t:128 * t + 128], ones[:, 0:1],
                                         start=True, stop=True)
                    last.then_inc(filled, 1)

                def scores(i):
                    pe.wait_ge(sem(tag + "_free_act"), turns[("q", 2 * i + 1, 1)][2])
                    if i >= 1:
                        pe.wait_ge(sem(tag + "_t"), i)
                    if layer == 0:
                        for a in range(2):
                            pe.wait_ge(sem("x0_kT"), 2 * (2 * i + a) + 2)
                            for b in range(B):
                                q = a * TOK + S * b
                                last = pe.matmul(ps[64 * (b % 2):64 * (b % 2) + 64, 4 + a,
                                                    S * (b // 2):S * (b // 2) + S],
                                                 q_T[:, q:q + S], k_T[a][:, S * b:S * b + S], start=True, stop=True)
                    else:
                        for b in range(B):
                            j, r, s = b // 4, b // 2 % 2, b % 2
                            c = S * (4 * j + 2 * s + r)
                            last = pe.matmul(pair(4)[:, c:c + S], q_T[:, 128 * b:128 * b + 128],
                                             ctxT[:, S * b:S * b + S], start=True, stop=True)
                    last.then_inc(sem(tag + "_s"), 1)

                def turn_probs(i):
                    pe.wait_ge(sem(tag + "_p"), i + 1)
                    for a in range(2):
                        b = bank(("pT", i, a))
                        for m in range(4):
                            c = 8 * a + 2 * m
                            last = pe.transpose(b[:, 128 * m:128 * m + 128],
                                                sm_t[:, c:c + 2, :].rearrange("p a b -> p (a b)"), ident[:, :])
                        last.then_inc(filled, 1)

                def context(i):
                    pe.wait_ge(sem(tag + "_free_dve"), turns[("pT", i, 1)][2])
                    for n in range(4):
                        b = bank(("o", i, n)).rearrange("p (a m q) -> p a m q", a=2, m=4)
                        r, jh = n % 2, n // 2
                        for m in range(4):
                            js = 4 * jh + m
                            if layer == 0:
                                mov = p_T[64 * r:64 * r + 64, :, S * js:S * js + S]
                            else:
                                mov = p_T.rearrange("p c (m a q) -> p (c m) a q", a=2, q=S)[64 * r:64 * r + 64, js]
                            last = pe.matmul(b[:, :, m, :], ctxn[64 * r:64 * r + 64, js, :], mov,
                                             start=True, stop=True)
                        last.then_inc(filled, 1)

                def project_out(i, half):
                    for t in range(4 * half, 4 * half + 4):
                        if t % 2 == 0:
                            pe.wait_ge(sem(tag + "_free_act"), turns[("o", i, 3)][2])
                        for a in range(2):
                            last = pe.matmul(tiles2(t // 2)[:, t % 2, :], o_T[:, a, 128 * t:128 * t + 128],
                                             wvo[:, 2 * i + a, :], start=(i == 0 and a == 0 and t % 2 == 0),
                                             stop=(i == NH // 2 - 1 and a == 1), skip_group_check=True)
                        if t % 2 and i == NH // 2 - 1:
                            last.then_inc(sem(tag + "_out"), 1)

                for i in range(NH // 2 + 2):
                    for a in range(2):
                        h = 2 * i + a
                        if h < NH:
                            queries(h)
                            if layer == 0:
                                keys(h)
                        if i >= 2:
                            project_out(i - 2, a)
                        if h < NH and layer == 0:
                            norms(h)
                    if 1 <= i <= NH // 2:
                        turn_probs(i - 1)
                    if i < NH // 2:
                        scores(i)
                    if 1 <= i <= NH // 2:
                        context(i - 1)

            norm_rows(1)
            cross(0)
            norm_rows(2)
            pe.wait_ge(sem("ld_f"), 48)
            for t in range(NT):
                for k in range(KH):
                    last = pe.matmul(ps[:, 7, 2 * t:2 * t + 2], xnT[:, k, 128 * t:128 * t + 128], f_router[:, k, :],
                                     start=(k == 0), stop=(k == KH - 1))
            last.then_inc(sem("f_logit"), 1)

            def hidden(n):
                c, e, hb = n // (2 * HB), n // HB % 2, n % HB
                if n == 3:
                    pe.wait_ge(sem("f_diff"), 1)
                if n >= 4:
                    pe.wait_ge(sem("f_leaky"), n - 3)
                for k in range(KH):
                    last = pe.matmul(ps[:, 4 + n % 4, :], f_fc[:, k, HID * e + 128 * hb:HID * e + 128 * hb + 128],
                                     xnT[:, k, c * HALF:c * HALF + HALF], start=(k == 0), stop=(k == KH - 1))
                last.then_inc(sem("f_h"), 1)

            def expert_out(n):
                e, hb = n // HB % 2, n % HB
                pe.wait_ge(sem("f_act"), n + 1)
                if n >= 2 * HB and hb == 0:
                    pe.wait_ge(sem("f_x"), n // HB - 1)
                for t in range(4):
                    last = pe.matmul(tiles2(2 * e + t // 2)[:, t % 2, :], f_act[n % 4][:, 128 * t:128 * t + 128],
                                     f_proj[:, HB * e + hb, :], start=(hb == 0 and t % 2 == 0),
                                     stop=(hb == HB - 1), skip_group_check=True)
                last.then_inc(sem("f_pr"), 1)

            for n in range(4 * HB + 2):
                if n < 4 * HB:
                    hidden(n)
                if n >= 2:
                    expert_out(n - 2)
            norm_rows(3)
            pe.wait_ge(sem("ld_a"), 80)
            for n in range(8):
                if n >= 4:
                    pe.wait_ge(sem("a_qk"), n - 3)
                for k in range(KH):
                    last = pe.matmul(ps[:, 4 + n % 4, :], a_wqkv[:, k, 128 * (n // 2):128 * (n // 2) + 128],
                                     xnT[:, k, HALF * (n % 2):HALF * (n % 2) + HALF],
                                     start=(k == 0), stop=(k == KH - 1))
                last.then_inc(sem("a_proj"), 1)
            for j in range(4):
                for s in range(2):
                    for r in range(2):
                        b = 4 * j + 2 * r + s
                        for k in range(KH):
                            last = pe.matmul(tiles2(j)[64 * r:64 * r + 64, s, :], xnT[:, k, S * b:S * b + S],
                                             a_wqkv[:, k, 2 * D:3 * D], start=(k == 0), stop=(k == KH - 1))
                last.then_inc(sem("a_vproj"), 1)
            for i in range(NH + 3):
                if i < NH:
                    pe.wait_ge(sem("a_qm"), i + 1)
                    pe.wait_ge(sem("a_qk"), 8)
                    if i >= 2:
                        pe.wait_ge(sem("a_t"), i - 1)
                    for b in range(B):
                        last = pe.matmul(ps[64 * (b % 2):64 * (b % 2) + 64, 4 + 2 * (i % 2),
                                            S * (b // 2):S * (b // 2) + S],
                                         a_qm[i % 2][:, S * b:S * b + S], a_k[:, i // 8, S * b:S * b + S],
                                         start=True, stop=True)
                    last.then_inc(sem("a_s"), 1)
                if i >= 3:
                    h = i - 3
                    pe.wait_ge(sem("a_pT"), h + 1)
                    pe.wait_ge(sem("a_v"), 4)
                    for r in range(2):
                        for j in range(4):
                            for s in range(2):
                                last = pe.matmul(ps[64 * s:64 * s + 64, 2 * r + j // 2,
                                                    256 * (j % 2) + HDS * h:256 * (j % 2) + HDS * h + HDS],
                                                 a_pT[64 * r:64 * r + 64, j, 64 * s:64 * s + 64],
                                                 a_v[64 * r:64 * r + 64, 2 * j + s, HDS * h:HDS * h + HDS],
                                                 start=True, stop=True)
                    last.then_inc(sem("a_ctx"), 1)
                if 2 <= i < NH + 2:
                    h = i - 2
                    pe.wait_ge(sem("a_p"), h + 1)
                    if h >= 1:
                        pe.wait_ge(sem("a_pT"), h)
                    for j in range(4):
                        last = pe.transpose(ps[:, 5, 128 * j:128 * j + 128],
                                            a_e[h % 2][:, 2 * j:2 * j + 2, :].rearrange("p a b -> p (a b)"),
                                            ident[:, :])
                    last.then_inc(sem("a_tr"), 1)
            for g in range(4):
                pe.wait_ge(sem("a_o"), 4)
                for k in range(KH):
                    for a in range(2):
                        last = pe.transpose(tiles2(4 + g)[:, k, 128 * a:128 * a + 128],
                                            a_o[:, 2 * g + a, 128 * k:128 * k + 128], ident[:, :])
                last.then_inc(sem("a_otr"), 1)
            for t in range(NT):
                pe.wait_ge(sem("a_oT"), t // 2 + 1)
                for k in range(KH):
                    last = pe.matmul(tiles2(t // 2)[:, t % 2, :], a_oT[:, k, 128 * t:128 * t + 128], a_wout[:, k, :],
                                     start=(k == 0), stop=(k == KH - 1))
                last.then_inc(sem("a_out"), 1)
            norm_rows(4)
            pe.wait_ge(sem("t_abs"), 3)
            pe.matmul(ps[:, 4, 0:3], ones[:, :], small[:, 8:11], start=True, stop=True).then_inc(sem("t_sum"), 1)
            pe.wait_ge(sem("t_ws"), 1)
            cross(1)
            for g in range(2):
                pe.wait_ge(sem("t_xq"), 1)
                xt = ps[:, 2 * g, :].bitcast(BF16).rearrange("p (k n) -> p k n", k=KH)
                for k in range(KH):
                    for t in range(4):
                        last = pe.transpose(xt[:, k, 128 * t:128 * t + 128],
                                            t_xq[:, 4 * g + t, 128 * k:128 * k + 128], identb[:, :])
                last.then_inc(sem("t_xtr"), 1)
            pe.wait_ge(sem("t_xT"), 2)
            pe.wait_ge(sem("t_wq"), 3)
            for t in range(NT + 1):
                if t < NT:
                    if t >= 1:
                        pe.wait_ge(sem("t_gate"), t)
                        pe.wait_ge(sem("t_prod"), t)
                    for o, w in ((0, t_gate_q), (2, t_up_q)):
                        for c in range(2):
                            for k in range(KH):
                                last = pe.matmul(ps[:, o + c, :], t_xqT[:, k, 128 * t:128 * t + 128],
                                                 w[:, k, 512 * c:512 * c + 512], start=(k == 0), stop=(k == KH - 1))
                    last.then_inc(sem("t_gu"), 1)
                if t >= 1:
                    pe.wait_ge(sem("t_hq"), t)
                    ht = ps[:, 4, :].bitcast(BF16)
                    for k in range(HB):
                        last = pe.transpose(ht[:, 128 * k:128 * k + 128], t_hq[(t - 1) % 2][:, 128 * k:128 * k + 128],
                                            identb[:, :])
                    last.then_inc(sem("t_htr"), 1)
                    pe.wait_ge(sem("t_hT"), t)
                    if t >= 3:
                        pe.wait_ge(sem("y_done"), t - 2)
                    for k in range(HB):
                        last = pe.matmul(ps[:, 5 + (t - 1) % 2, 0:D], t_hqT[:, k, :], t_down_q[:, k, :],
                                         start=(k == 0), stop=(k == HB - 1))
                    last.then_inc(sem("t_dn"), 1)

        @block.vector
        def _(dve):
            step = Counted(sem("dve_step"))

            def after(ins):
                step.on(ins)
                dve.wait_ge(step.sem, step.n)

            def norm_rows(ln, ready=None):
                def scale(g):
                    dve.wait_ge(sem("ln_rstd"), 4 * ln + g + 1)
                    for t in (2 * g, 2 * g + 1):
                        dve.tensor_scalar(xn[:, t, :], x[:, t, :], mv[:, t, 0:1], rstd[:, t:t + 1],
                                          ALU.subtract, ALU.mult).then_inc(sem("ln_xn"), 1)

                for g in range(4):
                    if ln == 0:
                        dve.wait_ge(sem(f"ld_rows{g}"), 16)
                    if ready is not None:
                        dve.wait_ge(ready[0], ready[1][g])
                        after(dve.tensor_tensor(x[:, 2 * g:2 * g + 2, :], tiles2(g), x[:, 2 * g:2 * g + 2, :],
                                                ALU.add))
                    for t in (2 * g, 2 * g + 1):
                        last = dve.bn_stats(stats[:, t, :], x[:, t, :])
                    after(last)
                    for t in (2 * g, 2 * g + 1):
                        last = dve.bn_aggr(mv[:, t, :], stats[:, t, :])
                    last.then_inc(sem("ln_var"), 1)
                    if g >= 1:
                        scale(g - 1)
                scale(3)

            dve.memset(eps_col, EPS)
            dve.memset(one_col, 1.0).then_inc(sem("ready"), 1)
            norm_rows(0)
            for i in range(2):
                after(dve.memset(m_da[i][:, :, 0:1], 0.0))
            dve.wait_ge(sem("ld_const"), 160)
            dve.tensor_scalar(mpar[:, :, 7:8], mpar[:, :, 6:7], 2.0, None, ALU.mult).then_inc(sem("m_b2"), 1)
            dve.wait_ge(sem("m_aexp"), 1)
            after(dve.tensor_scalar(a_log[:, :, :], a_log[:, :, :], -1.0, None, ALU.mult))

            def done(what, k):
                dve.wait_ge(sem("m_proj"), proj_no(what, k))
                return pair(proj_pair(what, k))

            def rest_of(src, rows, count):
                dve.wait_ge(sem("m_p0"), count + 1)
                dve.tensor_tensor(m_rest[0:rows], src[0:rows], m_part[0][0:rows], ALU.subtract)\
                    .then_inc(sem("m_r1"), 1)

            def last_part(rows, count):
                dve.wait_ge(sem("m_r1"), count + 1)
                dve.wait_ge(sem("m_p1"), count + 1)
                dve.tensor_tensor(m_part[2][0:rows], m_rest[0:rows], m_part[1][0:rows], ALU.subtract)\
                    .then_inc(sem("m_parts"), 1)

            def convolve(k):
                src = done("u", k)
                raw = src.rearrange("p (b t) -> p b t", t=S)
                acc = m_acc.rearrange("p (b t) -> p b t", t=S)
                if k:
                    dve.wait_ge(sem("m_u"), k)
                after(dve.tensor_scalar(m_acc, src, mpar[:, k, DCONV - 1:DCONV], None, ALU.mult))
                for lag in range(1, DCONV):
                    ins = dve.scalar_tensor_tensor(out=acc[:, :, lag:], in0=raw[:, :, :S - lag],
                                                   scalar=mpar[:, k, DCONV - 1 - lag:DCONV - lag],
                                                   in1=acc[:, :, lag:], op0=ALU.mult, op1=ALU.add)
                    if lag < DCONV - 1:
                        after(ins)
                ins.then_inc(sem("m_conv"), 1)

            def softplus(k):
                dve.wait_ge(sem("m_ln"), k + 1)
                poly, below = m_zs, m_rest
                after(dve.tensor_scalar(poly, m_e, 1.0 / 3.0, -0.5, ALU.mult, ALU.add))
                after(dve.tensor_tensor(poly, poly, m_e, ALU.mult))
                after(dve.scalar_tensor_tensor(out=poly, in0=poly, scalar=1.0, in1=m_e, op0=ALU.add, op1=ALU.mult))
                dve.wait_ge(sem("m_p1"), k + 1)
                after(dve.tensor_scalar(below, m_e, LOG1P_SPLIT, None, ALU.is_lt))
                after(dve.copy_predicated(m_ln, below.bitcast(mybir.dt.uint32), poly))
                if k >= 2:
                    dve.wait_ge(sem("m_da"), DST * (k - 1))
                dve.scalar_tensor_tensor(out=m_delta[k % 2].rearrange("p b t -> p (b t)"), in0=m_dtx, scalar=0.0,
                                         in1=m_ln, op0=ALU.max, op1=ALU.add).then_inc(sem("m_delta"), 1)

            def finish_block(k):
                dve.wait_ge(sem("m_y"), DST * (k + 1))
                dve.scalar_tensor_tensor(out=m_u[:, k, :], in0=m_u[:, k, :], scalar=mpar[:, k, 5:6], in1=pair(4),
                                         op0=ALU.mult, op1=ALU.add).then_inc(sem("m_yd"), 1)
                dve.wait_ge(sem("m_yd"), k + 1)
                dve.wait_ge(sem("m_zs"), k + 1)
                dve.tensor_tensor(m_u[:, k, :], m_u[:, k, :], m_zs, ALU.mult).then_inc(sem("m_yg"), 1)

            rest_of(pair(2), 64, 0)
            last_part(64, 0)
            convolve(0)
            rest_of(done("C", 0), 128, 1)
            last_part(128, 1)
            softplus(0)
            for u in range(NK * DST):
                k, n = u // DST, u % DST
                if n == 0:
                    dve.wait_ge(sem("m_u"), k + 1)
                    dve.wait_ge(sem("m_delta"), k + 1)
                    after(dve.tensor_tensor(m_du, m_delta[k % 2].rearrange("p b t -> p (b t)"), m_u[:, k, :],
                                            ALU.mult))
                dve.wait_ge(sem("m_b"), u + 1)
                dve.tensor_tensor(m_dbu[n % 2], pair(0), m_du, ALU.mult).then_inc(sem("m_dbu"), 1)
                dve.wait_ge(sem("m_dbu"), u + 1)
                dve.wait_ge(sem("m_da"), u + 1)
                dve.tensor_tensor_scan(m_h[n % 2], m_da[n % 2].rearrange("p b t -> p (b t)"), m_dbu[n % 2], 0.0,
                                       ALU.mult, ALU.add).then_inc(sem("m_scan"), 1)
                if n == 0 and k:
                    finish_block(k - 1)
                dve.wait_ge(sem("m_scan"), u + 1)
                dve.wait_ge(sem("m_c"), u + 1)
                if u >= 2:
                    dve.wait_ge(sem("m_y"), u - 1)
                dve.tensor_tensor(m_hc[n % 2], pair(2), m_h[n % 2], ALU.mult).then_inc(sem("m_hc"), 1)
                if k < NK - 1:
                    if n == 5:
                        convolve(k + 1)
                    if n == 7:
                        softplus(k + 1)
                    if n == 11:
                        rest_of(done("C", k + 1), 128, k + 2)
                    if n == 13:
                        last_part(128, k + 2)
            finish_block(NK - 1)

            def cross(layer):
                turns, tag = TURNS[layer], f"x{layer}"
                filled, freed = sem(tag + "_filled"), sem(tag + "_free_dve")

                def bank(job):
                    w = turns[job][0]
                    dve.wait_ge(filled, w + 1)
                    return ps[:, 6 + w % 2, :]

                for i in range(NH // 2):
                    b = bank(("wvo", i, 0))
                    dve.tensor_copy(wvo[:, 2 * i:2 * i + 2, :], b.rearrange("p (a n) -> p a n", a=2)).then_inc(freed, 1)
                top, den = small[:, 128:144], small[:, 144:160]

                def over_keys(col16):
                    return col16.unsqueeze(2).to_broadcast([128, B, S])

                def shift(i):
                    s = pair(4).rearrange("p (a b) -> p a b", b=S)
                    dve.wait_ge(sem(tag + "_s"), i + 1)
                    if layer == 0:
                        dve.wait_ge(sem("x0_rq"), 2 * i + 2)
                        ins = dve.tensor_tensor(sm_t, s, over_keys(small[:, 112:128]), ALU.mult)
                    else:
                        ins = dve.scalar_tensor_tensor(out=sm_t, in0=s, scalar=QSCALE, in1=mask_add,
                                                       op0=ALU.mult, op1=ALU.add)
                    ins.then_inc(sem(tag + "_t"), 1)
                    dve.wait_ge(sem(tag + "_t"), i + 1)
                    after(dve.tensor_reduce(top, sm_t, AX.X, ALU.max))
                    dve.tensor_tensor(sm_t, sm_t, over_keys(top), ALU.subtract).then_inc(sem(tag + "_shift"), 1)

                def divide(i):
                    dve.wait_ge(sem(tag + "_exp"), i + 1)
                    if layer == 1:
                        after(dve.tensor_tensor(sm_e, sm_e, mask_f, ALU.mult))
                    after(dve.tensor_reduce(den, sm_e, AX.X, ALU.add))
                    if layer == 1:
                        after(dve.tensor_scalar(den, den, 1e-30, None, ALU.max))
                    after(dve.reciprocal(den, den))
                    dve.tensor_tensor(sm_t, sm_e, over_keys(den), ALU.mult).then_inc(sem(tag + "_p"), 1)

                for i in range(NH // 2 + 1):
                    if i >= 1:
                        shift(i - 1)
                        divide(i - 1)
                    if i < NH // 2 and layer == 0:
                        for a in range(2):
                            for c in range(2):
                                cs = slice(c * HALF, c * HALF + HALF)
                                dve.wait_ge(sem("x0_rk"), 2 * (2 * i + a) + c + 1)
                                dve.tensor_tensor(k_T[a][:, cs], k_gain[:, cs], k_rn[:, cs], ALU.mult)\
                                    .then_inc(sem("x0_kT"), 1)
                    if i >= 1:
                        for a in range(2):
                            dve.tensor_copy(p_T[:, a, :], bank(("pT", i - 1, a))).then_inc(freed, 1)

            norm_rows(1, (sem("m_out"), [2, 4, 6, 8]))
            after(dve.tensor_tensor(g_col, gq_col, gk_col, ALU.mult))
            dve.tensor_scalar(g_col, g_col, QSCALE, None, ALU.mult).then_inc(sem("x0_g"), 1)
            cross(0)
            norm_rows(2, (sem("x0_out"), [1, 2, 3, 4]))
            lg = ps[:, 7, 0:2 * NT].rearrange("p (t e) -> p t e", e=2)
            dlt, mag, pick = small[:, 8:16], small[:, 16:24], small[:, 32:40]
            w_e = [small[:, 80:88], small[:, 88:96]]
            dve.wait_ge(sem("f_logit"), 1)
            after(dve.tensor_copy(dlt, lg[:, :, 0]))
            dve.tensor_tensor(dlt, dlt, lg[:, :, 1], ALU.subtract).then_inc(sem("f_diff"), 1)
            dve.wait_ge(sem("f_diff"), 1)
            after(dve.tensor_scalar(mag, dlt, -1.0, None, ALU.mult))
            dve.tensor_tensor(mag, mag, dlt, ALU.max).then_inc(sem("f_ld"), 1)
            after(dve.tensor_scalar(pick, dlt, 0.0, None, ALU.is_ge))
            dve.wait_ge(sem("f_e"), 1)
            after(dve.tensor_scalar(small[:, 24:32], small[:, 24:32], 1.0, None, ALU.add))
            after(dve.reciprocal(small[:, 24:32], small[:, 24:32]))
            after(dve.tensor_tensor(w_e[0], small[:, 24:32], pick, ALU.mult))
            after(dve.tensor_tensor(w_e[1], small[:, 24:32], w_e[0], ALU.subtract))
            for n in range(4 * HB):
                h = ps[:, 4 + n % 4, :]
                dve.wait_ge(sem("f_h"), n + 1)
                after(dve.tensor_scalar(f_neg[n % 2], h, 0.0, -0.5, ALU.min, ALU.mult))
                if n >= 2:
                    dve.wait_ge(sem("f_act"), n - 1)
                dve.tensor_tensor(f_leaky[n % 2], h, f_neg[n % 2], ALU.add).then_inc(sem("f_leaky"), 1)
                for m in ([n - 3] if n % HB == 3 and n > 3 else []) + ([n] if n == 4 * HB - 1 else []):
                    done = m // HB if m != n else 4
                    c, e = (done - 1) // 2, (done - 1) % 2
                    dve.wait_ge(sem("f_pr"), HB * done)
                    for t in range(4):
                        tt = 4 * c + t
                        ins = dve.scalar_tensor_tensor(out=x[:, tt, :], in0=tiles2(2 * e + t // 2)[:, t % 2, :],
                                                       scalar=w_e[e][:, tt:tt + 1], in1=x[:, tt, :],
                                                       op0=ALU.mult, op1=ALU.add)
                        if t == 3:
                            ins.then_inc(sem("f_x"), 1)
                            dve.wait_ge(sem("f_x"), done)
            norm_rows(3)
            dve.wait_ge(sem("ld_a"), 80)
            for j in range(4):
                dve.wait_ge(sem("a_vproj"), j + 1)
                dve.tensor_tensor(a_v[:, 2 * j:2 * j + 2, :], tiles2(j),
                                  a_bv.unsqueeze(1).to_broadcast([128, 2, D]), ALU.add).then_inc(sem("a_v"), 1)
            for t in range(NT):
                ins = dve.tensor_tensor(x[:, t, :], x[:, t, :], a_bo, ALU.add)
            after(ins)
            tops = [small[:, 56:64], small[:, 64:72]]
            dens2 = [small[:, 72:80], small[:, 80:88]]

            def a_divide(h):
                dve.wait_ge(sem("a_exp"), h + 1)
                e, dens = a_e[h % 2], dens2[h % 2]
                after(dve.tensor_reduce(dens, e, AX.X, ALU.add))
                after(dve.reciprocal(dens, dens))
                dve.tensor_tensor(e, e, spread(dens), ALU.mult).then_inc(sem("a_p"), 1)

            for h in range(NH):
                s = ps[:, 4 + 2 * (h % 2), :].rearrange("p (a b) -> p a b", b=S)
                t = a_t[h % 2]
                dve.wait_ge(sem("a_s"), h + 1)
                dve.scalar_tensor_tensor(out=t, in0=s, scalar=float(HDS) ** -0.5,
                                         in1=a_bias[:, h, :].unsqueeze(1).to_broadcast([128, NT, S]),
                                         op0=ALU.mult, op1=ALU.add).then_inc(sem("a_t"), 1)
                dve.wait_ge(sem("a_t"), h + 1)
                after(dve.tensor_reduce(tops[h % 2], t, AX.X, ALU.max))
                if h >= 2:
                    dve.wait_ge(sem("a_tr"), h - 1)
                dve.tensor_tensor(t, t, spread(tops[h % 2]), ALU.subtract).then_inc(sem("a_shift"), 1)
                if h >= 1:
                    a_divide(h - 1)
            a_divide(NH - 1)
            for g in range(4):
                r, j0 = g // 2, 2 * (g % 2)
                dve.wait_ge(sem("a_ctx"), NH)
                dve.tensor_copy(a_o.rearrange("p (j r) n -> p r j n", r=2)[:, r, j0:j0 + 2, :], tiles2(g))\
                    .then_inc(sem("a_o"), 1)
            norm_rows(4, (sem("a_out"), [2, 4, 6, 8]))
            dve.wait_ge(sem("ld_t"), 48)
            for i in range(3):
                dve.tensor_reduce(small[:, 8 + i:9 + i], t_w[i], AX.X, ALU.add, apply_absolute_value=True)\
                    .then_inc(sem("t_abs"), 1)
            ws, iws = small[:, 16:19], small[:, 19:22]
            dve.wait_ge(sem("t_sum"), 1)
            after(dve.tensor_scalar(ws, ps[:, 4, 0:3], 1.0 / (HID * D), EPS, ALU.mult, ALU.add))
            dve.reciprocal(iws, ws).then_inc(sem("t_ws"), 1)
            dve.wait_ge(sem("ld_x1m"), 16)
            for s in range(2):
                last = dve.tensor_copy(mask_f.rearrange("p (j s r) k -> p s j r k", s=2, r=2)[:, s],
                                       mask_u8.rearrange("p (j r s) k -> p s j r k", s=2, r=2)[:, s])
            after(last)
            after(dve.tensor_scalar(mask_add, mask_f, 1.0, -NEG, ALU.subtract, ALU.mult))
            cross(1)
            norm_rows(5, (sem("x1_out"), [1, 2, 3, 4]))
            dve.wait_ge(sem("ln_xn"), 48)
            xs, xrs = small[:, 24:32], small[:, 32:40]
            g_sc, u_sc = small[:, 56:64], small[:, 64:72]
            after(dve.tensor_reduce(xs, xn[:, :, :], AX.X, ALU.max, apply_absolute_value=True))
            after(dve.tensor_scalar(xs, xs, 1.0 / 127.0, EPS, ALU.mult, ALU.add))
            after(dve.reciprocal(xrs, xs))
            for t in range(NT):
                ins = dve.tensor_scalar(t_xr[:, t, :], xn[:, t, :], xrs[:, t:t + 1], 127.0, ALU.mult, ALU.min)
            after(ins)
            after(dve.tensor_scalar(t_xr, t_xr, -128.0, MAGIC, ALU.max, ALU.add))
            dve.tensor_scalar(t_xq, t_xr, MAGIC, None, ALU.subtract).then_inc(sem("t_xq"), 1)
            after(dve.tensor_scalar(g_sc, xs, ws[:, 0:1], None, ALU.mult))
            dve.tensor_scalar(u_sc, xs, ws[:, 1:2], None, ALU.mult).then_inc(sem("t_sc"), 1)
            dve.wait_ge(sem("t_sc"), 1)
            hs, hr, dn = small[:, 72:80], small[:, 80:88], small[:, 88:96]
            for t in range(NT + 1):
                if t < NT:
                    h = t_h[t % 2]
                    dve.wait_ge(sem("t_gate"), t + 1)
                    dve.scalar_tensor_tensor(out=h, in0=pair(2), scalar=u_sc[:, t:t + 1], in1=t_gate[t % 2],
                                             op0=ALU.mult, op1=ALU.mult).then_inc(sem("t_prod"), 1)
                    dve.wait_ge(sem("t_prod"), t + 1)
                    c = slice(t, t + 1)
                    after(dve.tensor_reduce(hs[:, c], h, AX.X, ALU.max, apply_absolute_value=True))
                    after(dve.tensor_scalar(hs[:, c], hs[:, c], 1.0 / 127.0, EPS, ALU.mult, ALU.add))
                    after(dve.reciprocal(hr[:, c], hs[:, c]))
                    after(dve.tensor_scalar(t_r, h, hr[:, c], 127.0, ALU.mult, ALU.min))
                    after(dve.tensor_scalar(t_r, t_r, -128.0, MAGIC, ALU.max, ALU.add))
                    if t >= 2:
                        dve.wait_ge(sem("t_htr"), t - 1)
                    dve.tensor_scalar(t_hq[t % 2], t_r, MAGIC, None, ALU.subtract).then_inc(sem("t_hq"), 1)
                    after(dve.tensor_tensor(dn[:, c], hs[:, c], ws[:, 2:3], ALU.mult))
                if t >= 1:
                    dve.wait_ge(sem("t_dn"), t)
                    dve.scalar_tensor_tensor(out=x[:, t - 1, :], in0=ps[:, 5 + (t - 1) % 2, 0:D],
                                             scalar=dn[:, t - 1:t], in1=x[:, t - 1, :],
                                             op0=ALU.mult, op1=ALU.add).then_inc(sem("y_done"), 1)


def layouts(i):
    import numpy as np

    def kparts(a):
        return a.reshape(-1, 128, a.shape[1]).transpose(1, 0, 2)

    def heads(a, n):
        return a.reshape(n, 128, a.shape[1]).transpose(1, 0, 2)

    w = i["L0_attn_W_in"]
    cut = np.cumsum([DI, DXB, DXB, DI])
    z, xb, bm, cm, dt = np.split(w, cut, axis=0)
    cm = cm.reshape(NK, 8, 4, 4, D).transpose(0, 2, 1, 3, 4).reshape(DI, D)
    xb = np.broadcast_to(xb.reshape(NK, 1, 16, D), (NK, 8, 16, D)).reshape(DI, D)
    win = np.concatenate([z, xb, bm, cm, dt], axis=0).T

    def chan(a):
        return a.reshape(NK, 128, -1).transpose(1, 0, 2)

    zero = np.zeros((DI, 1), np.float32)
    mpar = np.concatenate([i["L0_attn_conv_w"].reshape(DI, DCONV), i["L0_attn_conv_b"][:, None],
                           i["L0_attn_D_param"][:, None], i["L0_attn_b_dt"][:, None], zero], axis=1)
    ctx = i["ctx_1024"]
    ctxn = ctx.reshape(4, 2, 2, S, CD).transpose(1, 3, 0, 2, 4).reshape(128, NT, CD)
    row = np.arange(96)[:, None] % 32
    sel_b = np.repeat((row == np.arange(32)[None, :])[:, :, None], 128, axis=2)
    sel_c = row[:, :, None] == 4 * (np.arange(128)[None, None, :] // 16) + np.arange(4)[None, :, None]
    pos = np.arange(1 - S, 1)
    slope = 0.5 ** (np.arange(1, NH + 1) * (8.0 / NH))
    causal = np.arange(S)[None, None, :] <= (np.arange(128) % S)[:, None, None]
    a_bias = np.where(causal, (slope[:, None] * pos[None, :])[None], NEG)
    qkv, bqkv = i["L1_attn_Wqkv"], i["L1_attn_b_qkv"]
    bf16 = np.dtype("bfloat16")
    eye = np.eye(128)
    r = {
        "x": i["x"].reshape(NT, 128, D).transpose(1, 0, 2),
        "ctxT": ctx.reshape(TOK, CD).T, "ctxn": ctxn,
        "mask": np.asarray(i["mask_BxS2_bf1"]).view(np.uint8),
        "ident": eye.astype(np.float32), "identb": eye.astype(bf16), "ones": np.ones((128, 128), np.float32),
        "sel_b": sel_b.astype(bf16), "sel_c": sel_c.astype(bf16),
        "head_mask": (np.arange(128)[:, None] // HDS == np.arange(8)[None, :]).astype(np.float32),
        "a_bias": a_bias.astype(np.float32),
        "m_win": kparts(win), "m_wdt": i["L0_attn_W_dt"].T, "m_wout": kparts(i["L0_attn_W_out"].T),
        "a_log": chan(i["L0_attn_A_log"]), "mpar": chan(mpar),
        "g": np.stack([i["L0_xattn_gq"], i["L0_xattn_gk"]], axis=1),
        "x0_wq": kparts(i["L0_xattn_Wq"]), "x0_wk": i["L0_xattn_Wk"],
        "x0_wvT": i["L0_xattn_Wv"].reshape(CD, NH, HD).transpose(2, 1, 0), "x0_wo": heads(i["L0_xattn_Wo"], NH),
        "f_router": kparts(i["L0_ffn_w_router"].T),
        "f_fc": kparts(i["L0_ffn_w_fc"].reshape(2 * HID, D).T),
        "f_proj": kparts(i["L0_ffn_w_proj"].transpose(0, 2, 1).reshape(2 * HID, D)),
        "a_wqkv": kparts(qkv.T), "a_wout": kparts(i["L1_attn_Wout"].T),
        "a_bqk": bqkv[:2 * D].reshape(4, 128).T, "a_bv": bqkv[2 * D:], "a_bo": i["L1_attn_b_out"],
        "x1_wqT": i["L1_xattn_Wq"].reshape(D, NH, HD).transpose(2, 1, 0),
        "x1_wkT": i["L1_xattn_Wk"].reshape(CD, NKV, HD).transpose(2, 1, 0),
        "x1_wvT": i["L1_xattn_Wv"].reshape(CD, NKV, HD).transpose(2, 1, 0), "x1_wo": heads(i["L1_xattn_Wo"], NH),
        "t_gate": kparts(i["L1_ffn_w_gate"].T).reshape(128, -1), "t_up": kparts(i["L1_ffn_w_up"].T).reshape(128, -1),
        "t_down": kparts(i["L1_ffn_w_down"].T).reshape(128, -1),
    }
    return {k: np.ascontiguousarray(v) for k, v in r.items()}


def kernel(**inputs):
    import numpy as np
    import concourse.bacc as bacc
    from concourse.bass_utils import run_bass_kernel_spmd

    nc = bacc.Bacc("TRN2", target_bir_lowering=False, num_devices=1)
    arrays, io = {}, {}
    for name, a in layouts({k: np.asarray(v) for k, v in inputs.items()}).items():
        arrays[f"in_{name}"] = a
        io[name] = nc.dram_tensor(f"in_{name}", a.shape, mybir.dt.from_np(a.dtype), kind="ExternalInput").ap()
    out = nc.dram_tensor("out_x", (128, NT, D), F32, kind="ExternalOutput").ap()
    program(nc, io, out)
    got = run_bass_kernel_spmd(nc, [arrays], core_ids=[0]).results[0]["out_x"]
    return np.ascontiguousarray(np.asarray(got).transpose(1, 0, 2)).reshape(B, S, D)
```
